# Optimizing a Trainium2 kernel written in Bass

```python
import numpy as np
import jax
import jax.numpy as jnp

def _softmax(x, axis=-1):
    return jax.nn.softmax(x, axis=axis)

def _gelu(x):
    return jax.nn.gelu(x, approximate=True)

def _silu(x):
    return jax.nn.silu(x)

def _sigmoid(x):
    return jax.nn.sigmoid(x)

def _layernorm(x, axis=-1, eps=1e-05):
    m = jnp.mean(x, axis=axis, keepdims=True)
    v = jnp.var(x, axis=axis, keepdims=True)
    return (x - m) / jnp.sqrt(v + eps)

def _scatter_add(tgt, idx, src, axis=0):
    return tgt.at[idx].add(src)

def _segment_sum(src, seg, n):
    return jax.ops.segment_sum(src, seg, n)
kernel_name = 'mk_gnn_preln_d4_gnn_r8_104db3'

def setup_inputs(seed: int=0):
    np.random.seed(seed)
    _w = jnp.asarray

    def _rec_inputs():
        import jax
        import jax.numpy as jnp
        _gk = jax.random.key(seed)
        x = -0.000202 + 1 * jax.random.normal(jax.random.fold_in(_gk, 1), (6250, 128), jnp.float32)
        _s = jax.random.randint(jax.random.fold_in(_gk, 2), (50000,), 0, 6250, jnp.int32)
        _d = jax.random.randint(jax.random.fold_in(_gk, 3), (50000,), 0, 6250, jnp.int32)
        _loop = jnp.arange(6250, dtype=jnp.int32)
        src = jnp.concatenate([_s, _d, _loop])
        dst = jnp.concatenate([_d, _s, _loop])
        _o = jnp.argsort(dst, stable=True)
        src = src[_o]
        dst = dst[_o]
        edge_weight = jax.random.uniform(jax.random.fold_in(_gk, 13), (106250,), jnp.float32, 0.0, 0.999999)
        return (x, src, dst, edge_weight)
    x, src, dst, edge_weight = _rec_inputs()

    def _L0_gnn_setup():
        import jax, jax.numpy as jnp
        import numpy as np
        N, IN, H, D = (6250, 128, 4, 32)
        HID = H * D
        E = 100000
        key = jax.random.key(seed)
        ks = jax.random.split(key, 16)
        s_in = 1.0 / np.sqrt(IN)
        s_g = 1.0 / np.sqrt(3 * HID)
        inp = {'feat': jax.random.normal(ks[0], (N, IN), jnp.float32), 'src': jax.random.randint(ks[1], (E,), 0, N, jnp.int32), 'dst': jax.random.randint(ks[2], (E,), 0, N, jnp.int32), 'Wq': jax.random.normal(ks[3], (IN, HID), jnp.float32) * s_in, 'bq': jnp.zeros((HID,), jnp.float32), 'Wk': jax.random.normal(ks[4], (IN, HID), jnp.float32) * s_in, 'bk': jnp.zeros((HID,), jnp.float32), 'Wv': jax.random.normal(ks[5], (IN, HID), jnp.float32) * s_in, 'bv': jnp.zeros((HID,), jnp.float32), 'Ws': jax.random.normal(ks[6], (IN, HID), jnp.float32) * s_in, 'bs': jnp.zeros((HID,), jnp.float32), 'Wg': jax.random.normal(ks[7], (3 * HID, 1), jnp.float32) * s_g, 'bg': jnp.zeros((1,), jnp.float32), 'gamma': jnp.ones((HID,), jnp.float32), 'beta': jnp.zeros((HID,), jnp.float32), 'alpha': jnp.asarray(0.25, jnp.float32)}
        return inp
    _L0_gnn_all = _L0_gnn_setup()
    _L0_gnn_in = {k: v for k, v in _L0_gnn_all.items() if k in ('Wq', 'bq', 'Wk', 'bk', 'Wv', 'bv', 'Ws', 'bs', 'Wg', 'bg', 'gamma', 'beta', 'alpha')}
    del _L0_gnn_all

    def _L1_gnn_setup():
        import jax, jax.numpy as jnp
        import numpy as np
        N_NODES = 6250
        N_EDGES = 100000
        IN_CH = 128
        OUT_CH = 128
        MLP_HID = 64
        key = jax.random.key(seed)
        ks = jax.random.split(key, 8)
        x = jax.random.normal(ks[0], (N_NODES, IN_CH), dtype=jnp.float32)
        edge_index = jax.random.randint(ks[1], (2, N_EDGES), 0, N_NODES, dtype=jnp.int64)
        s1 = 1.0 / np.sqrt(2 * IN_CH)
        mlp_w1 = jax.random.uniform(ks[2], (2 * IN_CH, MLP_HID), jnp.float32, -s1, s1)
        mlp_b1 = jax.random.uniform(ks[3], (MLP_HID,), jnp.float32, -s1, s1)
        s2 = 1.0 / np.sqrt(MLP_HID)
        mlp_w2 = jax.random.uniform(ks[4], (MLP_HID, 1), jnp.float32, -s2, s2)
        mlp_b2 = jax.random.uniform(ks[5], (1,), jnp.float32, -s2, s2)
        s3 = 1.0 / np.sqrt(IN_CH)
        conv_w = jax.random.uniform(ks[6], (IN_CH, OUT_CH), jnp.float32, -s3, s3)
        conv_b = jnp.zeros((OUT_CH,), jnp.float32)
        return {'x': x, 'edge_index': edge_index, 'mlp_w1': mlp_w1, 'mlp_b1': mlp_b1, 'mlp_w2': mlp_w2, 'mlp_b2': mlp_b2, 'conv_w': conv_w, 'conv_b': conv_b}
    _L1_gnn_all = _L1_gnn_setup()
    _L1_gnn_in = {k: v for k, v in _L1_gnn_all.items() if k in ('mlp_w1', 'mlp_b1', 'mlp_w2', 'mlp_b2', 'conv_w', 'conv_b')}
    del _L1_gnn_all

    def _L2_gnn_setup():
        import jax, jax.numpy as jnp
        import numpy as np
        N_NODES = 6250
        N_EDGES = 100000
        D = 128

        def gcn_conv(x, edge_index, W, b):
            n = x.shape[0]
            loop = jnp.arange(n)
            row = jnp.concatenate([edge_index[0], loop])
            col = jnp.concatenate([edge_index[1], loop])
            deg = jnp.zeros((n,), dtype=x.dtype).at[col].add(1.0)
            deg_inv_sqrt = jnp.where(deg > 0, jax.lax.rsqrt(deg), 0.0)
            norm = deg_inv_sqrt[row] * deg_inv_sqrt[col]
            h = x @ W
            msg = h[row] * norm[:, None]
            out = jax.ops.segment_sum(msg, col, num_segments=n)
            return out + b
        key = jax.random.key(seed)
        k1, k2, k3, k4 = jax.random.split(key, 4)
        x = jax.random.normal(k1, (N_NODES, D), dtype=jnp.float32)
        edge_index = jax.random.randint(k2, (2, N_EDGES), 0, N_NODES, dtype=jnp.int64)
        scale = 1.0 / np.sqrt(D)
        W1 = jax.random.normal(k3, (D, D), dtype=jnp.float32) * scale
        W2 = jax.random.normal(k4, (D, D), dtype=jnp.float32) * scale
        b1 = jnp.zeros((D,), dtype=jnp.float32)
        b2 = jnp.zeros((D,), dtype=jnp.float32)
        return {'x': x, 'edge_index': edge_index, 'W1': W1, 'b1': b1, 'W2': W2, 'b2': b2}
    _L2_gnn_all = _L2_gnn_setup()
    _L2_gnn_in = {k: v for k, v in _L2_gnn_all.items() if k in ('W1', 'b1', 'W2', 'b2')}
    del _L2_gnn_all

    def _L3_gnn_setup():
        import jax, jax.numpy as jnp
        import numpy as np
        N = 12500
        E = 200000
        IN_F = 128
        OUT_F = 32
        H = 4
        NEG_SLOPE = 0.2
        key = jax.random.key(seed)
        ks = jax.random.split(key, 7)
        x = jax.random.normal(ks[0], (N, IN_F), dtype=jnp.float32)
        edge_index = jax.random.randint(ks[1], (2, E), 0, N, dtype=jnp.int64)
        edge_weight = jax.random.uniform(ks[2], (E,), dtype=jnp.float32)
        gain = np.sqrt(2.0)
        w_bound = gain * np.sqrt(6.0 / (IN_F + OUT_F))
        a_bound = gain * np.sqrt(6.0 / (OUT_F + 1))
        W = jax.random.uniform(ks[3], (H, IN_F, OUT_F), dtype=jnp.float32, minval=-w_bound, maxval=w_bound)
        a_l = jax.random.uniform(ks[4], (H, OUT_F, 1), dtype=jnp.float32, minval=-a_bound, maxval=a_bound)
        a_r = jax.random.uniform(ks[5], (H, OUT_F, 1), dtype=jnp.float32, minval=-a_bound, maxval=a_bound)
        bias = jnp.zeros((H * OUT_F,), dtype=jnp.float32)
        return {'x': x, 'edge_index': edge_index, 'edge_weight': edge_weight, 'W': W, 'a_l': a_l, 'a_r': a_r, 'bias': bias}
    _L3_gnn_all = _L3_gnn_setup()
    _L3_gnn_in = {k: v for k, v in _L3_gnn_all.items() if k in ('W', 'a_l', 'a_r', 'bias')}
    del _L3_gnn_all
    return {'x': x, 'src': src, 'dst': dst, 'edge_weight': edge_weight, 'L0_gnn_Wq': _L0_gnn_in['Wq'], 'L0_gnn_bq': _L0_gnn_in['bq'], 'L0_gnn_Wk': _L0_gnn_in['Wk'], 'L0_gnn_bk': _L0_gnn_in['bk'], 'L0_gnn_Wv': _L0_gnn_in['Wv'], 'L0_gnn_bv': _L0_gnn_in['bv'], 'L0_gnn_Ws': _L0_gnn_in['Ws'], 'L0_gnn_bs': _L0_gnn_in['bs'], 'L0_gnn_Wg': _L0_gnn_in['Wg'], 'L0_gnn_bg': _L0_gnn_in['bg'], 'L0_gnn_gamma': _L0_gnn_in['gamma'], 'L0_gnn_beta': _L0_gnn_in['beta'], 'L0_gnn_alpha': _L0_gnn_in['alpha'], 'L1_gnn_mlp_w1': _L1_gnn_in['mlp_w1'], 'L1_gnn_mlp_b1': _L1_gnn_in['mlp_b1'], 'L1_gnn_mlp_w2': _L1_gnn_in['mlp_w2'], 'L1_gnn_mlp_b2': _L1_gnn_in['mlp_b2'], 'L1_gnn_conv_w': _L1_gnn_in['conv_w'], 'L1_gnn_conv_b': _L1_gnn_in['conv_b'], 'L2_gnn_W1': _L2_gnn_in['W1'], 'L2_gnn_b1': _L2_gnn_in['b1'], 'L2_gnn_W2': _L2_gnn_in['W2'], 'L2_gnn_b2': _L2_gnn_in['b2'], 'L3_gnn_W': _L3_gnn_in['W'], 'L3_gnn_a_l': _L3_gnn_in['a_l'], 'L3_gnn_a_r': _L3_gnn_in['a_r'], 'L3_gnn_bias': _L3_gnn_in['bias']}

def reference(x, src, dst, edge_weight, L0_gnn_Wq, L0_gnn_bq, L0_gnn_Wk, L0_gnn_bk, L0_gnn_Wv, L0_gnn_bv, L0_gnn_Ws, L0_gnn_bs, L0_gnn_Wg, L0_gnn_bg, L0_gnn_gamma, L0_gnn_beta, L0_gnn_alpha, L1_gnn_mlp_w1, L1_gnn_mlp_b1, L1_gnn_mlp_w2, L1_gnn_mlp_b2, L1_gnn_conv_w, L1_gnn_conv_b, L2_gnn_W1, L2_gnn_b1, L2_gnn_W2, L2_gnn_b2, L3_gnn_W, L3_gnn_a_l, L3_gnn_a_r, L3_gnn_bias):
    import jax
    import jax.numpy as jnp

    def _L0_gnn_ref(feat, src, dst, Wq, bq, Wk, bk, Wv, bv, Ws, bs, Wg, bg, gamma, beta, alpha):
        import jax, jax.numpy as jnp
        import numpy as np
        N, IN, H, D = (6250, 128, 4, 32)
        HID = H * D
        E = 100000
        n = feat.shape[0]
        q = (feat @ Wq + bq).reshape(n, H, D)
        k = (feat @ Wk + bk).reshape(n, H, D)
        v = (feat @ Wv + bv).reshape(n, H, D)
        a = jnp.einsum('ehd,ehd->eh', q[src], k[dst]) / jnp.sqrt(jnp.float32(D))
        m = jax.ops.segment_max(a, dst, num_segments=n)
        m = jax.lax.stop_gradient(jnp.where(jnp.isfinite(m), m, 0.0))
        ex = jnp.exp(a - m[dst])
        denom = jax.ops.segment_sum(ex, dst, num_segments=n)
        denom = jnp.where(denom > 0, denom, 1.0)
        sa = ex / denom[dst]
        msg = v[src] * sa[:, :, None]
        agg = jax.ops.segment_sum(msg, dst, num_segments=n).reshape(n, HID)
        skip = feat @ Ws + bs
        g = jax.nn.sigmoid(jnp.concatenate([skip, agg, skip - agg], axis=-1) @ Wg + bg)
        rst = g * skip + (1.0 - g) * agg
        mu = rst.mean(-1, keepdims=True)
        var = rst.var(-1, keepdims=True)
        rst = (rst - mu) * jax.lax.rsqrt(var + 1e-05) * gamma + beta
        rst = jnp.where(rst >= 0, rst, alpha * rst)
        return rst

    def _L1_gnn_ref(x, edge_index, mlp_w1, mlp_b1, mlp_w2, mlp_b2, conv_w, conv_b):
        import jax, jax.numpy as jnp
        import numpy as np
        N_NODES = 6250
        N_EDGES = 100000
        IN_CH = 128
        OUT_CH = 128
        MLP_HID = 64
        n = x.shape[0]
        row, col = (edge_index[0], edge_index[1])
        edge_feat = jnp.concatenate([x[row], x[col]], axis=-1)
        h = jax.nn.gelu(edge_feat @ mlp_w1 + mlp_b1, approximate=False)
        edge_weight = jax.nn.sigmoid(h @ mlp_w2 + mlp_b2)[:, 0]
        loop = jnp.arange(n, dtype=row.dtype)
        row_f = jnp.concatenate([row, loop])
        col_f = jnp.concatenate([col, loop])
        ew_f = jnp.concatenate([edge_weight, jnp.ones((n,), x.dtype)])
        deg = jax.ops.segment_sum(ew_f, col_f, num_segments=n)
        dinv = jnp.where(deg > 0, jax.lax.rsqrt(deg), 0.0)
        norm = dinv[row_f] * ew_f * dinv[col_f]
        xt = x @ conv_w
        msg = xt[row_f] * norm[:, None]
        out = jax.ops.segment_sum(msg, col_f, num_segments=n)
        return out + conv_b

    def _L2_gnn_ref(x, edge_index, W1, b1, W2, b2):
        import jax, jax.numpy as jnp
        import numpy as np
        N_NODES = 6250
        N_EDGES = 100000
        D = 128

        def gcn_conv(x, edge_index, W, b):
            n = x.shape[0]
            loop = jnp.arange(n)
            row = jnp.concatenate([edge_index[0], loop])
            col = jnp.concatenate([edge_index[1], loop])
            deg = jnp.zeros((n,), dtype=x.dtype).at[col].add(1.0)
            deg_inv_sqrt = jnp.where(deg > 0, jax.lax.rsqrt(deg), 0.0)
            norm = deg_inv_sqrt[row] * deg_inv_sqrt[col]
            h = x @ W
            msg = h[row] * norm[:, None]
            out = jax.ops.segment_sum(msg, col, num_segments=n)
            return out + b
        h = gcn_conv(x, edge_index, W1, b1)
        h = gcn_conv(h, edge_index, W2, b2)
        return jax.nn.leaky_relu(h, negative_slope=0.1)

    def _L3_gnn_ref(x, edge_index, edge_weight, W, a_l, a_r, bias):
        import jax, jax.numpy as jnp
        import numpy as np
        N = 12500
        E = 200000
        IN_F = 128
        OUT_F = 32
        H = 4
        NEG_SLOPE = 0.2
        n = x.shape[0]
        row, col = (edge_index[0], edge_index[1])
        Wh = jnp.einsum('ni,hio->hno', x, W)
        e_l = jnp.einsum('hno,ho->hn', Wh, a_l[..., 0])
        e_r = jnp.einsum('hno,ho->hn', Wh, a_r[..., 0])
        e = e_l[:, row] + e_r[:, col]
        e = jax.nn.leaky_relu(e, negative_slope=NEG_SLOPE)
        e = e + jnp.log(jnp.clip(edge_weight, 1e-08, None))[None, :]
        eT = e.T
        e_max = jax.ops.segment_max(eT, col, num_segments=n)
        alpha = jnp.exp(eT - e_max[col])
        alpha_sum = jax.ops.segment_sum(alpha, col, num_segments=n)
        alpha = alpha / (alpha_sum[col] + 1e-08)
        msgs = alpha[:, :, None] * jnp.transpose(Wh, (1, 0, 2))[row]
        out = jax.ops.segment_sum(msgs, col, num_segments=n)
        out = out.reshape(n, -1) + bias
        return out
    edge_index = jnp.stack([src, dst])
    h = jnp.maximum(_layernorm(x, axis=-1), 0.0)
    x = x + _L0_gnn_ref(h, src, dst, L0_gnn_Wq, L0_gnn_bq, L0_gnn_Wk, L0_gnn_bk, L0_gnn_Wv, L0_gnn_bv, L0_gnn_Ws, L0_gnn_bs, L0_gnn_Wg, L0_gnn_bg, L0_gnn_gamma, L0_gnn_beta, L0_gnn_alpha)
    h = jnp.maximum(_layernorm(x, axis=-1), 0.0)
    x = x + _L1_gnn_ref(h, edge_index, L1_gnn_mlp_w1, L1_gnn_mlp_b1, L1_gnn_mlp_w2, L1_gnn_mlp_b2, L1_gnn_conv_w, L1_gnn_conv_b)
    h = jnp.maximum(_layernorm(x, axis=-1), 0.0)
    x = x + _L2_gnn_ref(h, edge_index, L2_gnn_W1, L2_gnn_b1, L2_gnn_W2, L2_gnn_b2)
    h = jnp.maximum(_layernorm(x, axis=-1), 0.0)
    x = x + _L3_gnn_ref(h, edge_index, edge_weight, L3_gnn_W, L3_gnn_a_l, L3_gnn_a_r, L3_gnn_bias)
    return x

_drawn_inputs = setup_inputs


def setup_inputs(seed=0):
    import zlib

    import numpy as np

    out = dict(_drawn_inputs(seed))
    spreads = {'L0_gnn_bq': (0.0, 2.0),
     'L0_gnn_bk': (0.0, 0.8),
     'L0_gnn_bv': (0.0, 0.1),
     'L0_gnn_bs': (0.0, 0.1),
     'L0_gnn_gamma': (1.0, 0.2),
     'L0_gnn_beta': (0.0, 0.1),
     'L1_gnn_conv_b': (0.0, 0.1),
     'L2_gnn_b1': (0.0, 0.1),
     'L2_gnn_b2': (0.0, 0.1),
     'L3_gnn_bias': (0.0, 0.1)}
    factors = {'L1_gnn_mlp_w1': 8.0, 'L1_gnn_mlp_b1': 26.837, 'L1_gnn_mlp_w2': 8.0}
    for name, (base, spread) in spreads.items():
        noise = np.random.default_rng([zlib.crc32(name.encode()), seed]).standard_normal(out[name].shape)
        drawn = base * np.exp(spread * noise) if base else spread * noise
        out[name] = jnp.asarray(drawn.astype(out[name].dtype))
    for name, factor in factors.items():
        out[name] = (out[name] * factor).astype(out[name].dtype)
    return out
```

```python
import concourse.bass as bass
from concourse import mybir
from contextlib import ExitStack

fp32 = mybir.dt.float32
i32 = mybir.dt.int32
ALU = mybir.AluOpType
ACT = mybir.ActivationFunctionType
AX = mybir.AxisListType.X

P = 128
N = 6250
E = 106250
F = 128
H = 4
D = F // H
NB = -(-N // P)
NTAIL = N - (NB - 1) * P
NPAD = NB * P
TB = 8
T = -(-E // (P * 32)) * 32
EP = T * P
BATCHES = T // TB
ROUNDS = BATCHES // 2
ROWS = NPAD + P
GB = 7
GROUPS = NB // GB
CH = 32
CT = T // CH
CE = CT * P
BIG = 1e30
SCALE = 1.0 / float(D) ** 0.5
assert NB % GB == 0 and T % CH == 0 and BATCHES % 2 == 0


class Chain:

    def __init__(self, eng, sem, start=0):
        self.eng, self.sem, self.start, self.n = eng, sem, start, 0

    def link(self, ins):
        self.n += 1
        ins.then_inc(self.sem, 1)
        self.eng.wait_ge(self.sem, self.start + self.n)


class Phase(ExitStack):

    def __init__(self, nc):
        super().__init__()
        self.nc, self.sems = nc, []

    def __exit__(self, *exc):
        if self.sems and exc[0] is None:
            self.nc.clear_and_free_semaphores(self.sems)
            self.nc.all_engine_barrier()
        return super().__exit__(*exc)


def gnn_kernel(nc, a, out):
    ctx = ExitStack()

    def sb(name, shape, dt=fp32, where=None):
        return (where or ctx).enter_context(nc.sbuf_tensor(name, shape, dt))

    def ps(where, name, shape):
        return where.enter_context(nc.psum_tensor(name, shape, fp32))

    def sem(where, name):
        s = nc.alloc_semaphore(name)
        where.sems.append(s)
        return s

    def dram(name, shape):
        return nc.dram_tensor(name, shape, fp32, kind="Internal").ap()

    tab_qv = dram("tab_qv", [ROWS, 2 * F])
    tab_k = dram("tab_k", [ROWS, F])
    tab_a = dram("tab_a", [ROWS, F // 2])
    tab_b = dram("tab_b", [ROWS, F // 2])
    tab_row = dram("tab_row", [ROWS, F])
    tab_wh = dram("tab_wh", [ROWS, F + H])
    tab_er = dram("tab_er", [ROWS, H])
    spill = dram("spill", [P, T, F])

    with ctx:
        x_nat = sb("x_nat", [P, NB, F])
        keep = sb("keep", [P, NB, F])
        acc = sb("acc", [P, ROWS])
        score = sb("score", [P, H * T])
        local = sb("local", [P, T + TB])
        src_idx = sb("src_idx", [P, T], i32)
        base = sb("base", [1, T + TB], i32)
        iota = sb("iota", [P, P])
        ident = sb("ident", [P, P])
        dinv = sb("dinv", [P, 2 * NB])
        w_cat = sb("w_cat", [P, 4 * F])
        b_cat = sb("b_cat", [P, 3 * F])
        wg = sb("wg", [P, 3, F])
        wgs = sb("wgs", [P, 2, F])
        ones = sb("ones", [1, 1])
        vec = sb("vec", [P, 4, F])
        col = sb("col", [P, 4])

        def of_batch(n):
            return score[:].rearrange("p (h t) -> p t h", h=H)[:, bass.ds(n * TB, TB), :]

        def bcast(v, n):
            return bass.AP(tensor=v.tensor, offset=v.offset, ap=[[0, P], [1, n]])

        with Phase(nc) as cx:
            dst_pt = sb("dst_pt", [P, T], i32, cx)
            base_all = sb("base_all", [P, T], i32, cx)
            zero = sb("zero", [P, 2 * F], fp32, cx)
            s_in = sem(cx, "s_in")
            s_zero = sem(cx, "s_zero")
            s_pad = sem(cx, "s_pad")
            s_io = sem(cx, "s_io")
            s_set = sem(cx, "s_set")
            with nc.Block() as block:
                @block.sync
                def _(sp):
                    sp.dma_start(dst_pt[:], a["dst_pt"]).then_inc(s_in, 16)
                    sp.dma_start(base_all[:], bass.AP(tensor=a["dst_pt"].tensor, offset=0, ap=[[0, P], [1, T]])
                                 ).then_inc(s_in, 16)
                    sp.dma_start(src_idx[:], a["src_pt"]).then_inc(s_in, 16)
                    sp.wait_ge(s_zero, 1)
                    sp.dma_start(x_nat[:, 0:NB - 1, :], a["x"][0:(NB - 1) * P, :].rearrange("(b p) f -> p b f", p=P)
                                 ).then_inc(s_in, 16)
                    sp.dma_start(x_nat[0:NTAIL, NB - 1, :], a["x"][(NB - 1) * P:N, :]).then_inc(s_in, 16)
                    tabs = (tab_qv, tab_k, tab_a, tab_b, tab_row, tab_wh, tab_er)
                    for t in tabs:
                        sp.dma_start(t[NPAD:ROWS, :], zero[:, 0:t.shape[1]]).then_inc(s_pad, 16)
                    sp.wait_ge(s_pad, 16 * len(tabs))
                    sp.wait_ge(s_in, 16 * 5)

                @block.gpsimd
                def _(pool):
                    nc.gpsimd.iota(iota[:], [[1, P]], base=0, channel_multiplier=0,
                                   allow_small_or_imprecise_dtypes=True).then_inc(s_io, 1)
                    nc.gpsimd.memset(ident[:], 0.0).then_inc(s_io, 1)
                    pool.wait_ge(s_io, 2)
                    nc.gpsimd.affine_select(out=ident[:], in_=ident[:], compare_op=ALU.not_equal, fill=1.0,
                                            base=0, pattern=[[-1, P]], channel_multiplier=1).then_inc(s_io, 1)

                @block.vector
                def _(dve):
                    nc.vector.memset(x_nat[:, NB - 1, :], 0.0)
                    nc.vector.memset(zero[:], 0.0).then_inc(s_zero, 1)
                    nc.vector.memset(local[:], 0.0)
                    nc.vector.memset(base[:], 0)
                    nc.vector.memset(ones[:], 1.0).then_inc(s_set, 1)
                    dve.wait_ge(s_in, 16 * 5)
                    dve.wait_ge(s_set, 1)
                    nc.vector.tensor_tensor(local[:, 0:T], dst_pt[:], base_all[:], ALU.subtract)
                    nc.vector.tensor_copy(base[0:1, 0:T], dst_pt[0:1, :])

        def onehot(dst, n):
            return nc.vector.tensor_tensor(dst, iota[:].unsqueeze(1).to_broadcast([P, TB, P]),
                                           local[:, bass.ds(n * TB, TB)].unsqueeze(2).to_broadcast([P, TB, P]),
                                           ALU.is_equal)

        def score_pass(layer):
            table, win = {0: (tab_qv, tab_k), 1: (tab_a, tab_b), 3: (tab_wh, tab_er)}[layer]
            RW, WW = table.shape[1], win.shape[1]
            spills = layer != 1
            v0 = F if layer == 0 else 0
            with Phase(nc) as cx:
                L = f"l{layer}_"
                idx = sb(L + "idx", [P, 2 * TB], i32, cx)
                rows = sb(L + "rows", [P, 2 * TB, RW], fp32, cx)
                hot = sb(L + "hot", [P, 2, TB, P], fp32, cx)
                hotT = sb(L + "hotT", [P, 2, TB, P], fp32, cx)
                winr = sb(L + "winr", [P, 2 * TB, WW], fp32, cx)
                pT = ps(cx, L + "pT", [P, TB, P])
                pK = ps(cx, L + "pK", [P, 2, TB, WW])
                s_rows = [sem(cx, L + f"s_rows{b}") for b in range(2)]
                s_win = [sem(cx, L + f"s_win{b}") for b in range(2)]
                s_spill = [sem(cx, L + f"s_spill{b}") for b in range(2)]
                s_idx = sem(cx, L + "s_idx")
                s_used = sem(cx, L + "s_used")
                s_hot = sem(cx, L + "s_hot")
                s_tr = sem(cx, L + "s_tr")
                s_hotT = sem(cx, L + "s_hotT")
                s_dst = sem(cx, L + "s_dst")
                s_chain = sem(cx, L + "s_chain")
                s_ew = sem(cx, L + "s_ew")
                if layer == 1:
                    pre = sb(L + "pre", [P, 2, TB, WW], fp32, cx)
                    act = sb(L + "act", [P, 2, TB, WW], fp32, cx)
                    logit = sb(L + "logit", [P, 2, TB], fp32, cx)
                    lo = sb(L + "lo", [P, 2, TB, P], fp32, cx)
                    hi = sb(L + "hi", [P, 2, TB, 2 * NB], fp32, cx)
                    dst_i = sb(L + "dst_i", [P, T], i32, cx)
                    dst_d = sb(L + "dst_d", [P, T], i32, cx)
                    dlo = sb(L + "dlo", [P, T], fp32, cx)
                    dhi = sb(L + "dhi", [P, T], fp32, cx)
                    zer = sb(L + "zer", [P, P], fp32, cx)
                    pD = ps(cx, L + "pD", [P, 2 * NB])
                    s_dl = sem(cx, L + "s_dl")
                    s_pre = s_used
                    s_act = sem(cx, L + "s_act")
                    s_logit = sem(cx, L + "s_logit")
                    s_edge = sem(cx, L + "s_edge")
                    s_hi = sem(cx, L + "s_hi")
                    s_deg = sem(cx, L + "s_deg")
                    s_dend = sem(cx, L + "s_dend")
                    s_sqrt = sem(cx, L + "s_sqrt")
                    s_zer = sem(cx, L + "s_zer")
                if layer == 0:
                    prod = sb(L + "prod", [P, 2, TB, F], fp32, cx)
                if layer == 3:
                    lin = sb(L + "lin", [P, 2, TB, H], fp32, cx)
                    lnw = sb(L + "lnw", [P, T], fp32, cx)
                    s_lin = sem(cx, L + "s_lin")
                    s_lnc = sem(cx, L + "s_lnc")
                    s_lnw = sem(cx, L + "s_lnw")

                with nc.Block() as block:
                    @block.sync
                    def _(sp):
                        if layer == 1:
                            sp.dma_start(dst_i[:], a["dst_pt"]).then_inc(s_dl, 16)
                            sp.sem_inc(s_deg, 2)
                        if layer == 3:
                            sp.dma_start(lnw[:], a["ew_pt"]).then_inc(s_ew, 16)
                        sp.sem_inc(s_dst, 2)
                        for b in range(2):
                            sp.sem_inc(s_spill[b], 16)
                        regs = [sp.alloc_register(L + f"win{u}") for u in range(TB)]

                        def load_windows(n, b):
                            sp.load(regs, base[0:1, bass.ds(n * TB, TB)])
                            sp.wait_ge(s_dst, n + 1)
                            for u in range(TB):
                                at = sp.snap(regs[u], min_val=0, max_val=N)
                                sp.dma_start(winr[:, b * TB + u, :], win[bass.ds(at, P), :]).then_inc(s_win[b], 16)

                        def store_values(n, b, i):
                            sp.wait_ge(s_rows[b], i * (16 * TB) + 16 * TB)
                            sp.dma_start(spill[:, bass.ds(n * TB, TB), :], rows[:, b * TB:(b + 1) * TB, v0:v0 + F]
                                         ).then_inc(s_spill[b], 16)

                        load_windows(0, 0)
                        with sp.Fori(0, ROUNDS) as i:
                            for b in range(2):
                                load_windows(i * 2 + b + 1, 1 - b)
                                if spills:
                                    store_values(i * 2 + b, b, i)
                        if spills:
                            for b in range(2):
                                sp.wait_ge(s_spill[b], 16 * (ROUNDS + 1))
                        sp.wait_ge(s_win[0], 16 * TB * (ROUNDS + 1))

                    @block.gpsimd
                    def _(pool):
                        pool.sem_inc(s_used, 2)
                        with pool.Fori(0, ROUNDS) as i:
                            for b in range(2):
                                pool.wait_ge(s_used, i * 2 + b + 1)
                                if spills:
                                    pool.wait_ge(s_spill[b], i * 16 + 16)
                                nc.gpsimd.tensor_copy(idx[:, b * TB:(b + 1) * TB],
                                                      src_idx[:, bass.ds((i * 2 + b) * TB, TB)]).then_inc(s_idx, 1)
                                pool.wait_ge(s_idx, 1)
                                pool.wait_ge(s_idx, i * 2 + b + 1)
                                for u in range(b * TB, (b + 1) * TB):
                                    nc.gpsimd.indirect_dma_start(
                                        rows[:, u, :], None, table,
                                        bass.IndirectOffsetOnAxis(idx[:, u:u + 1], 0)).then_inc(s_rows[b], 16)

                    @block.tensor
                    def _(pe):
                        def turn(n, b):
                            pe.wait_ge(s_hot, n + 1)
                            for u in range(TB):
                                last = nc.tensor.transpose(pT[:, u, :], hot[:, b, u, :], ident[:])
                            last.then_inc(s_tr, 1)

                        if layer == 1:
                            pe.wait_ge(s_zer, 1)
                            nc.tensor.matmul(pD[:], zer[:], zer[:, 0:2 * NB], start=True, stop=False)
                        turn(0, 0)
                        with pe.Fori(0, ROUNDS) as i:
                            for b in range(2):
                                n = i * 2 + b
                                pe.wait_ge(s_hotT, n + 1)
                                turn(n + 1, 1 - b)
                                pe.wait_ge(s_win[b], i * (16 * TB) + 16 * TB)
                                pe.wait_ge(s_used, n + 1)
                                for u in range(TB):
                                    last = nc.tensor.matmul(pK[:, b, u, :], hotT[:, b, u, :], winr[:, b * TB + u, :],
                                                            start=True, stop=True)
                                last.then_inc(s_dst, 1)
                                if layer == 1:
                                    pe.wait_ge(s_hi, n + 1)
                                    for u in range(TB):
                                        last = nc.tensor.matmul(pD[:], lo[:, b, u, :], hi[:, b, u, :],
                                                                start=False, stop=False)
                                    last.then_inc(s_deg, 1)
                        if layer == 1:
                            nc.tensor.matmul(pD[:], zer[:], zer[:, 0:2 * NB], start=False, stop=True
                                             ).then_inc(s_dend, 1)

                    @block.scalar
                    def _(act_e):
                        def copy_turned(n, b):
                            act_e.wait_ge(s_tr, n + 1)
                            act_e.wait_ge(s_dst, n + 1)
                            nc.scalar.activation(hotT[:, b, 0:4, :], pT[:, 0:4, :], ACT.Copy)
                            nc.scalar.activation(hotT[:, b, 4:8, :], pT[:, 4:8, :], ACT.Copy).then_inc(s_hotT, 1)

                        if layer == 3:
                            act_e.wait_ge(s_lnc, 1)
                            nc.scalar.activation(lnw[:], lnw[:], ACT.Ln).then_inc(s_lnw, 1)
                        copy_turned(0, 0)
                        with act_e.Fori(0, ROUNDS) as i:
                            for b in range(2):
                                n = i * 2 + b
                                copy_turned(n + 1, 1 - b)
                                if layer == 1:
                                    act_e.wait_ge(s_pre, n + 3)
                                    nc.scalar.activation(act[:, b], pre[:, b], ACT.Gelu).then_inc(s_act, 1)
                                    act_e.wait_ge(s_logit, n + 1)
                                    nc.scalar.activation(score[:, bass.ds(n * TB, TB)], logit[:, b], ACT.Sigmoid,
                                                         bias=col[:, 0:1]).then_inc(s_edge, 1)
                        if layer == 1:
                            act_e.wait_ge(s_dend, 2)
                            nc.scalar.activation(dinv[:], dinv[:], ACT.Sqrt).then_inc(s_sqrt, 1)

                    @block.vector
                    def _(dve):
                        if layer == 1:
                            nc.vector.memset(zer[:], 0.0).then_inc(s_zer, 1)
                            dve.wait_ge(s_dl, 16)
                            pc = Chain(dve, s_ew)
                            pc.link(nc.vector.tensor_scalar(dst_d[:], dst_i[:], P - 1, None, ALU.bitwise_and))
                            pc.link(nc.vector.tensor_copy(dlo[:], dst_d[:]))
                            pc.link(nc.vector.tensor_scalar(dst_d[:], dst_i[:], 7, None, ALU.logical_shift_right))
                            pc.link(nc.vector.tensor_copy(dhi[:], dst_d[:]))
                        if layer == 3:
                            dve.wait_ge(s_ew, 16)
                            nc.vector.tensor_scalar(lnw[:], lnw[:], 1e-8, None, ALU.max).then_inc(s_lnc, 1)
                            dve.wait_ge(s_lnw, 1)
                        onehot(hot[:, 0], 0).then_inc(s_hot, 1)
                        with dve.Fori(0, ROUNDS) as i:
                            for b in range(2):
                                n = i * 2 + b
                                rb = rows[:, b * TB:(b + 1) * TB, :]
                                dve.wait_ge(s_dst, n + 2)
                                onehot(hot[:, 1 - b], n + 1).then_inc(s_hot, 1)
                                dve.wait_ge(s_dst, n + 3)
                                dve.wait_ge(s_rows[b], i * (16 * TB) + 16 * TB)
                                if layer == 0:
                                    for g in range(2):
                                        last = nc.vector.tensor_tensor(prod[:, b, 4 * g:4 * g + 4, :],
                                                                       rb[:, 4 * g:4 * g + 4, 0:F],
                                                                       pK[:, b, 4 * g:4 * g + 4, :], ALU.mult)
                                        last.then_inc(s_chain, 1)
                                    dve.wait_ge(s_chain, 2)
                                    dve.wait_ge(s_chain, n * 2 + 2)
                                    nc.vector.tensor_reduce(
                                        of_batch(n), prod[:, b].rearrange("p t (h d) -> p t h d", d=D), AX, ALU.add
                                    ).then_inc(s_used, 1)
                                if layer == 1:
                                    nc.vector.tensor_tensor(pre[:, b], rb, pK[:, b], ALU.add).then_inc(s_pre, 1)
                                    if b == 0:
                                        dve.wait_ge(s_deg, n + 1)
                                    else:
                                        dve.wait_ge(s_deg, n + 1)
                                    nc.vector.tensor_tensor(
                                        lo[:, b], iota[:].unsqueeze(1).to_broadcast([P, TB, P]),
                                        dlo[:, bass.ds(n * TB, TB)].unsqueeze(2).to_broadcast([P, TB, P]), ALU.is_equal)
                                    nc.vector.tensor_tensor(
                                        hi[:, b, :, NB:2 * NB], iota[:, 0:NB].unsqueeze(1).to_broadcast([P, TB, NB]),
                                        dhi[:, bass.ds(n * TB, TB)].unsqueeze(2).to_broadcast([P, TB, NB]),
                                        ALU.is_equal)
                                    dve.wait_ge(s_act, n + 1)
                                    nc.vector.tensor_tensor(
                                        act[:, b], act[:, b],
                                        vec[:, 0, 0:WW].unsqueeze(1).to_broadcast([P, TB, WW]), ALU.mult
                                    ).then_inc(s_chain, 1)
                                    dve.wait_ge(s_chain, n + 1)
                                    nc.vector.tensor_reduce(logit[:, b], act[:, b], AX, ALU.add).then_inc(s_logit, 1)
                                    dve.wait_ge(s_edge, n + 1)
                                    nc.vector.tensor_tensor(
                                        hi[:, b, :, 0:NB], hi[:, b, :, NB:2 * NB],
                                        score[:, bass.ds(n * TB, TB)].unsqueeze(2).to_broadcast([P, TB, NB]),
                                        ALU.mult).then_inc(s_hi, 1)
                                if layer == 3:
                                    nc.vector.tensor_tensor(lin[:, b], rb[:, :, F:F + H], pK[:, b], ALU.add
                                                            ).then_inc(s_chain, 1)
                                    dve.wait_ge(s_chain, n * 2 + 1)
                                    nc.vector.scalar_tensor_tensor(lin[:, b], lin[:, b], 0.2, lin[:, b],
                                                                   ALU.mult, ALU.max).then_inc(s_chain, 1)
                                    dve.wait_ge(s_chain, n * 2 + 2)
                                    nc.vector.tensor_tensor(
                                        of_batch(n), lin[:, b],
                                        lnw[:, bass.ds(n * TB, TB)].unsqueeze(2).to_broadcast([P, TB, H]), ALU.add
                                    ).then_inc(s_used, 1)
                        if layer == 1:
                            dve.wait_ge(s_dend, 1)
                            nc.vector.tensor_scalar(dinv[:], pD[:], 1.0, None, ALU.add).then_inc(s_dend, 1)
                            dve.wait_ge(s_sqrt, 1)
                            nc.vector.reciprocal(dinv[:], dinv[:])

        def softmax(layer):
            scale, eps = (SCALE, 0.0) if layer == 0 else (1.0, 1e-8)
            with Phase(nc) as cx:
                L = f"x{layer}_"
                dchunk = sb(L + "dchunk", [P, CE + 2], i32, cx)
                same = sb(L + "same", [P, CE + 1], fp32, cx)
                brk = sb(L + "brk", [P, CE + 1], fp32, cx)
                lg = sb(L + "lg", [P, CE], fp32, cx)
                fw = sb(L + "fw", [P, CE], fp32, cx)
                bw = sb(L + "bw", [P, CE], fp32, cx)
                whole = sb(L + "whole", [P, 2], fp32, cx)
                rowg = sb(L + "rowg", [1, 2, P], fp32, cx)
                rowp = sb(L + "rowp", [1, 2, P], fp32, cx)
                carry = sb(L + "carry", [1, 4, P + 1], fp32, cx)
                init = sb(L + "init", [P, 4], fp32, cx)
                pB = ps(cx, L + "pB", [P, CT, P])
                pR = ps(cx, L + "pR", [P, 4 * P])
                s_dc = sem(cx, L + "s_dc")
                s_turn = sem(cx, L + "s_turn")
                s_lg = sem(cx, L + "s_lg")
                s_whole = sem(cx, L + "s_whole")
                s_rowg = sem(cx, L + "s_rowg")
                s_end = sem(cx, L + "s_end")
                s_row = sem(cx, L + "s_row")
                s_car = sem(cx, L + "s_car")
                s_init = sem(cx, L + "s_init")
                s_c = sem(cx, L + "s_c")
                s_exp = sem(cx, L + "s_exp")
                s_diff = sem(cx, L + "s_diff")
                s_w = sem(cx, L + "s_w")
                s_back = sem(cx, L + "s_back")
                by_chunk = score[:].rearrange("p (q j) -> p j q", j=CT)
                ends = [(fw, CE - 1), (bw, 0), (fw, CE - 1), (bw, 0)]
                with nc.Block() as block:
                    @block.sync
                    def _(sp):
                        for h in range(H):
                            sp.dma_start(dchunk[h * CH:(h + 1) * CH, :],
                                         bass.AP(tensor=a["dst_line"].tensor, offset=0, ap=[[CE, CH], [1, CE + 2]])
                                         ).then_inc(s_dc, 16)
                        sp.wait_ge(s_dc, 16 * H)

                    @block.tensor
                    def _(pe):
                        for j in range(CT):
                            last = nc.tensor.transpose(pB[:, j, :], by_chunk[:, j], ident[:])
                        last.then_inc(s_turn, 1)
                        pe.wait_ge(s_whole, 1)
                        for k in range(2):
                            last = nc.tensor.matmul(pR[0:1, k * P:(k + 1) * P], whole[:, k:k + 1], ident[:],
                                                    start=True, stop=True)
                        last.then_inc(s_rowg, 1)
                        for k, (buf, at) in enumerate(ends):
                            pe.wait_ge(s_end, k + 1)
                            nc.tensor.matmul(pR[0:1, 2 * P:3 * P], buf[:, at:at + 1], ident[:], start=True, stop=True
                                             ).then_inc(s_row, 1)
                            pe.wait_ge(s_car, k + 1)
                            o = k % 2
                            nc.tensor.matmul(pR[:, 3 * P:3 * P + 1], carry[0:1, k, o:o + P], ones[:],
                                             start=True, stop=True).then_inc(s_init, 1)
                        pe.wait_ge(s_w, 1)
                        for j in range(CT):
                            last = nc.tensor.transpose(pB[:, j, :], lg[:, j * P:(j + 1) * P], ident[:])
                        last.then_inc(s_back, 1)

                    @block.scalar
                    def _(act_e):
                        act_e.wait_ge(s_turn, 1)
                        for j in range(0, CT, 4):
                            m = min(4, CT - j)
                            last = nc.scalar.activation(lg[:, j * P:(j + m) * P].rearrange("p (j e) -> p j e", e=P),
                                                        pB[:, j:j + m, :], ACT.Copy)
                        last.then_inc(s_lg, 1)
                        act_e.wait_ge(s_diff, 1)
                        nc.scalar.activation(lg[:], lg[:], ACT.Exp, scale=scale).then_inc(s_exp, 1)
                        act_e.wait_ge(s_back, 1)
                        for j in range(0, CT, 4):
                            m = min(4, CT - j)
                            nc.scalar.activation(by_chunk[:, j:j + m], pB[:, j:j + m, :], ACT.Copy)

                    @block.vector
                    def _(dve):
                        c = Chain(dve, s_c)
                        dve.wait_ge(s_dc, 16 * H)
                        c.link(nc.vector.tensor_tensor(same[:], dchunk[:, 0:CE + 1], dchunk[:, 1:CE + 2], ALU.is_equal))
                        nc.vector.tensor_reduce(whole[:, 0:1], same[:, 0:CE], AX, ALU.min)
                        nc.vector.tensor_reduce(whole[:, 1:2], same[:, 1:CE + 1], AX, ALU.min).then_inc(s_whole, 1)
                        nc.vector.tensor_scalar(brk[:], same[:], 1.0, BIG, ALU.subtract, ALU.mult)
                        nc.vector.memset(carry[:], -BIG)
                        dve.wait_ge(s_rowg, 1)
                        c.link(nc.vector.tensor_copy(rowg[:].rearrange("p k n -> p (k n)"), pR[0:1, 0:2 * P]))
                        c.link(nc.vector.tensor_scalar(rowp[:], rowg[:], 1.0, BIG, ALU.subtract, ALU.mult))
                        c.link(nc.vector.memset(carry[:, 2, :], 0.0))

                        def segment_scan(k, out, data, marks, rows_, op0, op1, start):
                            back = k % 2
                            m = marks[:, 1:CE + 1] if back else marks[:, 0:CE]
                            rev = (lambda ap: ap[:, ::-1]) if back else (lambda ap: ap)
                            nc.vector.tensor_tensor_scan(rev(out), rev(m), rev(data), start, op0, op1
                                                         ).then_inc(s_end, 1)
                            dve.wait_ge(s_row, k + 1)
                            row = pR[0:1, 2 * P:3 * P]
                            to = carry[:, k, 0:P] if back else carry[:, k, 1:P + 1]
                            nc.vector.tensor_tensor_scan(rev(to), rev(rows_[:, back, :]), rev(row), start, op0, op1
                                                         ).then_inc(s_car, 1)
                            dve.wait_ge(s_init, k + 1)
                            c.link(nc.vector.tensor_copy(init[:, k:k + 1], pR[:, 3 * P:3 * P + 1]))
                            c.link(nc.vector.tensor_tensor_scan(rev(out), rev(m), rev(data), init[:, k:k + 1],
                                                                op0, op1))

                        dve.wait_ge(s_lg, 1)
                        segment_scan(0, fw[:], lg[:], brk, rowp, ALU.add, ALU.max, -BIG)
                        segment_scan(1, bw[:], fw[:], brk, rowp, ALU.add, ALU.max, -BIG)
                        nc.vector.tensor_tensor(lg[:], lg[:], bw[:], ALU.subtract).then_inc(s_diff, 1)
                        dve.wait_ge(s_exp, 1)
                        segment_scan(2, fw[:], lg[:], same, rowg, ALU.mult, ALU.add, 0.0)
                        segment_scan(3, bw[:], fw[:], brk, rowp, ALU.add, ALU.max, -BIG)
                        if eps:
                            c.link(nc.vector.tensor_scalar(bw[:], bw[:], eps, None, ALU.add))
                        c.link(nc.vector.reciprocal(bw[:], bw[:]))
                        nc.vector.tensor_tensor(lg[:], lg[:], bw[:], ALU.mult).then_inc(s_w, 1)

        def aggregate(name, weights, gather):
            with Phase(nc) as cx:
                L = name + "_"
                hot = sb(L + "hot", [P, 2, TB, P], fp32, cx)
                rows = sb(L + "rows", [P, 2 * TB, F], fp32, cx)
                idx = sb(L + "idx", [P, 2 * TB], i32, cx)
                wrow = sb(L + "wrow", [P, 2 * TB, F], fp32, cx) if weights else rows
                pA = ps(cx, L + "pA", [P, 2, TB, P])
                s_rows = [sem(cx, L + f"s_rows{b}") for b in range(2)]
                s_idx = sem(cx, L + "s_idx")
                s_hot = sem(cx, L + "s_hot")
                s_sum = sem(cx, L + "s_sum")
                s_free = s_hot if weights else s_sum
                s_add = sem(cx, L + "s_add")
                with nc.Block() as block:
                    @block.gpsimd
                    def _(pool):
                        pool.sem_inc(s_hot, 2)
                        if gather:
                            with pool.Fori(0, ROUNDS) as i:
                                for b in range(2):
                                    pool.wait_ge(s_free, i * 2 + b + 1)
                                    nc.gpsimd.tensor_copy(idx[:, b * TB:(b + 1) * TB],
                                                          src_idx[:, bass.ds((i * 2 + b) * TB, TB)]).then_inc(s_idx, 1)
                                    pool.wait_ge(s_idx, 1)
                                    pool.wait_ge(s_idx, i * 2 + b + 1)
                                    for u in range(b * TB, (b + 1) * TB):
                                        nc.gpsimd.indirect_dma_start(
                                            rows[:, u, :], None, tab_row,
                                            bass.IndirectOffsetOnAxis(idx[:, u:u + 1], 0)).then_inc(s_rows[b], 16)

                    @block.sync
                    def _(sp):
                        if not gather:
                            with sp.Fori(0, ROUNDS) as i:
                                for b in range(2):
                                    sp.wait_ge(s_free, i * 2 + b + 1)
                                    sp.dma_start(rows[:, b * TB:(b + 1) * TB, :],
                                                 spill[:, bass.ds((i * 2 + b) * TB, TB), :]).then_inc(s_rows[b], 16)

                    per_batch = 16 * TB if gather else 16

                    @block.tensor
                    def _(pe):
                        with pe.Fori(0, ROUNDS) as i:
                            for b in range(2):
                                n = i * 2 + b
                                pe.wait_ge(s_hot, n + 3)
                                if not weights:
                                    pe.wait_ge(s_rows[b], i * per_batch + per_batch)
                                for u in range(TB):
                                    last = nc.tensor.matmul(pA[:, b, u, :], wrow[:, b * TB + u, :], hot[:, b, u, :],
                                                            start=True, stop=True)
                                last.then_inc(s_sum, 1)

                    @block.vector
                    def _(dve):
                        regs = [dve.alloc_register(L + f"at{u}") for u in range(TB)]

                        def prepare(n, b, i):
                            dve.wait_ge(s_sum, n + 1)
                            one = onehot(hot[:, b], n)
                            if not weights:
                                one.then_inc(s_hot, 1)
                                return
                            dve.wait_ge(s_rows[b], i * per_batch + per_batch)
                            if weights == H:
                                last = nc.vector.tensor_tensor(
                                    wrow[:, b * TB:(b + 1) * TB, :].rearrange("p t (h d) -> p t h d", d=D),
                                    rows[:, b * TB:(b + 1) * TB, :].rearrange("p t (h d) -> p t h d", d=D),
                                    of_batch(n).unsqueeze(3).to_broadcast([P, TB, H, D]),
                                    ALU.mult)
                            else:
                                last = nc.vector.tensor_tensor(
                                    wrow[:, b * TB:(b + 1) * TB, :], rows[:, b * TB:(b + 1) * TB, :],
                                    score[:, bass.ds(n * TB, TB)].unsqueeze(2).to_broadcast([P, TB, F]), ALU.mult)
                            last.then_inc(s_hot, 1)

                        def add_windows(n, b):
                            dve.load(regs, base[0:1, bass.ds(n * TB, TB)])
                            dve.wait_ge(s_sum, n + 3)
                            for u in range(TB):
                                at = dve.snap(regs[u], min_val=0, max_val=N)
                                dve.wait_ge(s_add, n * TB + u + 1)
                                nc.vector.tensor_tensor(acc[:, bass.ds(at, P)], acc[:, bass.ds(at, P)],
                                                        pA[:, b, u, :], ALU.add).then_inc(s_add, 1)

                        dve.sem_inc(s_sum, 2)
                        nc.vector.memset(acc[:], 0.0).then_inc(s_add, 1)
                        prepare(0, 0, 0)
                        with dve.Fori(0, ROUNDS - 1) as i:
                            prepare(i * 2 + 1, 1, i)
                            add_windows(i * 2, 0)
                            prepare(i * 2 + 2, 0, i + 1)
                            add_windows(i * 2 + 1, 1)
                        prepare(BATCHES - 1, 1, ROUNDS - 1)
                        add_windows(BATCHES - 2, 0)
                        add_windows(BATCHES - 1, 1)

        def node_phase(kind):
            cols = {"in": 4 * F, "gate": 2 * F, "gcn": F, "mid": F, "gat": F, "out": 0}[kind]
            has_acc = kind != "in"
            norm = kind in ("in", "gate", "gcn", "gat")
            loads = {
                "in": [(w_cat[:, k * F:(k + 1) * F], a[n]) for k, n in enumerate(("L0_gnn_Wq", "L0_gnn_Wv", "L0_gnn_Wk", "L0_gnn_Ws"))]
                + [(b_cat[:, k * F:(k + 1) * F], bcast(a[n], F)) for k, n in enumerate(("L0_gnn_bq", "L0_gnn_bv", "L0_gnn_bk"))]
                + [(vec[:, 0, :], bcast(a["L0_gnn_bs"], F))],
                "gate": [(w_cat[:, 0:F // 2], a["L1_gnn_mlp_w1"][0:F, :]), (w_cat[:, F // 2:F], a["L1_gnn_mlp_w1"][F:2 * F, :]),
                         (w_cat[:, F:2 * F], a["L1_gnn_conv_w"]), (b_cat[:, 0:F // 2], bcast(a["L1_gnn_mlp_b1"], F // 2)),
                         (wg[:].rearrange("p k f -> p (k f)"), bcast(a["L0_gnn_Wg"], 3 * F)),
                         (col[:, 0:1], bcast(a["L1_gnn_mlp_b2"], 1)), (col[:, 1:2], bcast(a["L0_gnn_bg"], 1)),
                         (col[:, 2:3], bcast(a["L0_gnn_alpha"], 1)), (vec[:, 0, 0:F // 2], bcast(a["L1_gnn_mlp_w2"], F // 2)),
                         (vec[:, 1, :], bcast(a["L0_gnn_gamma"], F)), (vec[:, 2, :], bcast(a["L0_gnn_beta"], F))],
                "gcn": [(w_cat[:, 0:F], a["L2_gnn_W1"]), (vec[:, 1, :], bcast(a["L1_gnn_conv_b"], F))],
                "mid": [(w_cat[:, 0:F], a["L2_gnn_W2"]), (vec[:, 1, :], bcast(a["L2_gnn_b1"], F))],
                "gat": [(w_cat[:, h * D:(h + 1) * D], a["L3_gnn_W"][h]) for h in range(H)]
                + [(vec[:, 1, :], bcast(a["L2_gnn_b2"], F)), (vec[:, 2, :], bcast(a["L3_gnn_a_l"], F)),
                   (vec[:, 3, :], bcast(a["L3_gnn_a_r"], F))],
                "out": [(vec[:, 1, :], bcast(a["L3_gnn_bias"], F))],
            }[kind]
            W1 = F if kind == "gat" else cols
            with Phase(nc) as cx:
                L = kind + "_"
                xin = sb(L + "xin", [P, GB, F], fp32, cx)
                hb = sb(L + "hb", [P, GB, F], fp32, cx)
                tmp = sb(L + "tmp", [P, GB, F], fp32, cx)
                tm2 = sb(L + "tm2", [P, GB, F], fp32, cx)
                accs = sb(L + "accs", [P, GB * P], fp32, cx)
                agg = sb(L + "agg", [P, GB, F], fp32, cx)
                hT = sb(L + "hT", [P, GB * P], fp32, cx)
                st = sb(L + "st", [P, 4, GB], fp32, cx)
                slab = sb(L + "slab", [P, GB, 3 * F], fp32, cx)
                er = sb(L + "er", [P, 2, GB, H], fp32, cx)
                pX = ps(cx, L + "pX", [P, 8, P])
                pG = ps(cx, L + "pG", [P, 2, 4 * F])
                s_ld = sem(cx, L + "s_ld")
                s_c = sem(cx, L + "s_c")
                s_pc = sem(cx, L + "s_pc")
                s_stage = sem(cx, L + "s_stage")
                s_aggT = sem(cx, L + "s_aggT")
                s_agg = sem(cx, L + "s_agg")
                s_var = sem(cx, L + "s_var")
                s_std = sem(cx, L + "s_std")
                s_z = sem(cx, L + "s_z")
                s_gate = sem(cx, L + "s_gate")
                s_h = sem(cx, L + "s_h")
                s_ht = sem(cx, L + "s_ht")
                s_hT = sem(cx, L + "s_hT")
                s_mm = sem(cx, L + "s_mm")
                s_ev = sem(cx, L + "s_ev")
                s_slab = sem(cx, L + "s_slab")
                s_done = sem(cx, L + "s_done")
                s_st = sem(cx, L + "s_st")
                norms = 2 if kind == "gate" else int(norm)

                def rows_of(table, i, c0, c1):
                    return table[0:NPAD, c0:c1].rearrange("(b p) c -> p b c", p=P)[:, bass.ds(i * GB, GB), :]

                stores = {
                    "in": [(tab_qv, 0, 2 * F, slab[:, :, 0:2 * F]), (tab_k, 0, F, slab[:, :, 2 * F:3 * F])],
                    "gate": [(tab_a, 0, F // 2, slab[:, :, 0:F // 2]), (tab_b, 0, F // 2, slab[:, :, F // 2:F])],
                    "gcn": [(tab_row, 0, F, slab[:, :, 0:F])], "mid": [(tab_row, 0, F, slab[:, :, 0:F])],
                    "gat": [(tab_wh, 0, F, slab[:, :, 0:F]), (tab_wh, F, F + H, er[:, 0]), (tab_er, 0, H, er[:, 1])],
                    "out": [],
                }[kind]
                with nc.Block() as block:
                    @block.sync
                    def _(sp):
                        for to, of in loads:
                            sp.dma_start(to, of).then_inc(s_ld, 16)
                        sp.sem_inc(s_st, 16)
                        if stores:
                            with sp.Fori(0, GROUPS) as i:
                                if kind == "gat":
                                    sp.wait_ge(s_slab, i + 1)
                                else:
                                    sp.wait_ge(s_ev, i * GB + GB + 2)
                                for table, c0, c1, of in stores:
                                    sp.dma_start(rows_of(table, i, c0, c1), of).then_inc(s_st, 16)
                            sp.wait_ge(s_st, 16 + 16 * GROUPS * len(stores))
                        else:
                            sp.wait_ge(s_slab, GROUPS)
                            sp.dma_start(out[0:(NB - 1) * P, :].rearrange("(b p) f -> p b f", p=P),
                                         x_nat[:, 0:NB - 1, :]).then_inc(s_st, 16)
                            sp.dma_start(out[(NB - 1) * P:N, :], x_nat[0:NTAIL, NB - 1, :]).then_inc(s_st, 16)
                            sp.wait_ge(s_st, 16 * 3)
                        sp.wait_ge(s_ld, 16 * len(loads))

                    @block.scalar
                    def _(ae):
                        with ae.Fori(0, GROUPS) as i:
                            if has_acc:
                                nc.scalar.activation(accs[:], acc[:, bass.ds(i * (GB * P), GB * P)], ACT.Copy
                                                     ).then_inc(s_stage, 1)
                                ae.wait_ge(s_aggT, i + 1)
                                nc.scalar.activation(agg[:, 0:4, :], pX[:, 0:4, :], ACT.Copy)
                                nc.scalar.activation(agg[:, 4:GB, :], pX[:, 4:GB, :], ACT.Copy).then_inc(s_agg, 1)
                            if kind == "gate":
                                ae.wait_ge(s_z, i + 1)
                                nc.scalar.activation(st[:, 3, :], st[:, 2, :], ACT.Sigmoid, bias=col[:, 1:2]
                                                     ).then_inc(s_gate, 1)
                            for k in range(norms):
                                ae.wait_ge(s_var, i * norms + k + 1)
                                nc.scalar.activation(st[:, 1, :], st[:, 1, :], ACT.Sqrt).then_inc(s_std, 1)
                            if cols:
                                ae.wait_ge(s_ht, i + 1)
                                nc.scalar.activation(hT[:, 0:4 * P].rearrange("p (u n) -> p u n", n=P),
                                                     pX[:, 0:4, :], ACT.Copy)
                                nc.scalar.activation(hT[:, 4 * P:GB * P].rearrange("p (u n) -> p u n", n=P),
                                                     pX[:, 4:GB, :], ACT.Copy).then_inc(s_hT, 1)
                                ae.wait_ge(s_mm, i * GB + GB)
                            else:
                                ae.wait_ge(s_slab, i + 1)

                    @block.tensor
                    def _(pe):
                        pe.wait_ge(s_ld, 16 * len(loads))
                        with pe.Fori(0, GROUPS) as i:
                            if has_acc:
                                pe.wait_ge(s_stage, i + 1)
                                for u in range(GB):
                                    last = nc.tensor.transpose(pX[:, u, :], accs[:, u * P:(u + 1) * P], ident[:])
                                last.then_inc(s_aggT, 1)
                            if cols:
                                pe.wait_ge(s_h, i + 1)
                                for u in range(GB):
                                    last = nc.tensor.transpose(pX[:, u, :], hb[:, u, :], ident[:])
                                last.then_inc(s_ht, 1)
                                pe.wait_ge(s_hT, i + 1)
                                for u in range(GB):
                                    pe.wait_ge(s_ev, i * GB + u + 1)
                                    nc.tensor.matmul(pG[:, u % 2, 0:cols], hT[:, u * P:(u + 1) * P], w_cat[:, 0:cols],
                                                     start=True, stop=True).then_inc(s_mm, 1)

                    @block.vector
                    def _(dve):
                        dve.wait_ge(s_ld, 16 * len(loads))
                        dve.sem_inc(s_ev, 2)
                        if kind == "gate":
                            nc.vector.tensor_tensor(wgs[:, 0, :], wg[:, 0, :], wg[:, 2, :], ALU.add)
                            pc = Chain(dve, s_pc)
                            pc.link(nc.vector.tensor_tensor(wgs[:, 1, :], wg[:, 1, :], wg[:, 2, :], ALU.subtract))

                        steps = {"in": 7, "gate": 24, "gcn": 11, "mid": 2, "gat": 14, "out": 1}[kind]

                        def over_blocks(v):
                            return v.unsqueeze(1).to_broadcast([P, GB, F])

                        def over_feats(s):
                            return s.unsqueeze(2).to_broadcast([P, GB, F])

                        with dve.Fori(0, GROUPS) as i:
                            c = Chain(dve, s_c, i * steps)
                            xi = x_nat[:, bass.ds(i * GB, GB), :]
                            ki = keep[:, bass.ds(i * GB, GB), :]

                            def layer_norm(to, of, k):
                                c.link(nc.vector.tensor_reduce(st[:, 0, :], of, AX, ALU.add))
                                c.link(nc.vector.tensor_scalar(st[:, 0, :], st[:, 0, :], 1.0 / F, None, ALU.mult))
                                c.link(nc.vector.tensor_tensor(to, of, over_feats(st[:, 0, :]), ALU.subtract))
                                c.link(nc.vector.tensor_tensor(tmp[:], to, to, ALU.mult))
                                c.link(nc.vector.tensor_reduce(st[:, 1, :], tmp[:], AX, ALU.add))
                                nc.vector.tensor_scalar(st[:, 1, :], st[:, 1, :], 1.0 / F, 1e-5, ALU.mult, ALU.add
                                                        ).then_inc(s_var, 1)
                                dve.wait_ge(s_std, i * norms + k + 1)
                                c.link(nc.vector.reciprocal(st[:, 1, :], st[:, 1, :]))
                                return nc.vector.tensor_tensor(to, to, over_feats(st[:, 1, :]), ALU.mult)

                            if has_acc:
                                dve.wait_ge(s_agg, i + 1)
                            if kind == "gate":
                                nc.vector.tensor_tensor(tmp[:], ki, over_blocks(wgs[:, 0, :]), ALU.mult)
                                c.link(nc.vector.tensor_tensor(tm2[:], agg[:], over_blocks(wgs[:, 1, :]), ALU.mult))
                                c.link(nc.vector.tensor_tensor(tmp[:], tmp[:], tm2[:], ALU.add))
                                nc.vector.tensor_reduce(st[:, 2, :], tmp[:], AX, ALU.add).then_inc(s_z, 1)
                                c.link(nc.vector.tensor_tensor(xin[:], ki, agg[:], ALU.subtract))
                                dve.wait_ge(s_gate, i + 1)
                                c.link(nc.vector.tensor_tensor(xin[:], xin[:], over_feats(st[:, 3, :]), ALU.mult))
                                c.link(nc.vector.tensor_tensor(xin[:], xin[:], agg[:], ALU.add))
                                c.link(layer_norm(tm2[:], xin[:], 0))
                                c.link(nc.vector.tensor_tensor(tm2[:], tm2[:], over_blocks(vec[:, 1, :]), ALU.mult))
                                c.link(nc.vector.tensor_tensor(tm2[:], tm2[:], over_blocks(vec[:, 2, :]), ALU.add))
                                c.link(nc.vector.tensor_scalar(tmp[:], tm2[:], 0.0, col[:, 2:3], ALU.min, ALU.mult))
                                c.link(nc.vector.scalar_tensor_tensor(tm2[:], tm2[:], 0.0, tmp[:], ALU.max, ALU.add))
                                nc.vector.tensor_tensor(xin[:], xi, tm2[:], ALU.add)
                                c.link(nc.vector.tensor_tensor(xi, xi, tm2[:], ALU.add))
                            if kind in ("gcn", "mid", "gat"):
                                k = 0 if kind == "gcn" else 1
                                di = dinv[:, bass.ds(i * GB + k * NB, GB)]
                                c.link(nc.vector.tensor_tensor(tmp[:], agg[:], ki, ALU.add))
                                c.link(nc.vector.tensor_tensor(tmp[:], tmp[:], over_feats(di), ALU.mult))
                                last = nc.vector.tensor_tensor(hb[:] if kind == "mid" else tmp[:], tmp[:],
                                                               over_blocks(vec[:, 1, :]), ALU.add)
                                if kind == "mid":
                                    last.then_inc(s_h, 1)
                                else:
                                    c.link(last)
                                if kind == "gat":
                                    c.link(nc.vector.scalar_tensor_tensor(tmp[:], tmp[:], 0.1, tmp[:], ALU.mult, ALU.max))
                                if kind != "mid":
                                    nc.vector.tensor_tensor(xin[:], xi, tmp[:], ALU.add)
                                    c.link(nc.vector.tensor_tensor(xi, xi, tmp[:], ALU.add))
                            if kind == "out":
                                c.link(nc.vector.tensor_tensor(agg[:], agg[:], over_blocks(vec[:, 1, :]), ALU.add))
                                nc.vector.tensor_tensor(xi, xi, agg[:], ALU.add).then_inc(s_slab, 1)
                            if norm:
                                c.link(layer_norm(hb[:], xi if kind == "in" else xin[:], norms - 1))
                                nc.vector.tensor_scalar(hb[:], hb[:], 0.0, None, ALU.max).then_inc(s_h, 1)
                            if cols:
                                dve.wait_ge(s_st, i * (16 * len(stores)) + 16)
                                for u in range(GB):
                                    dve.wait_ge(s_mm, i * GB + u + 1)
                                    g = pG[:, u % 2, :]
                                    own = keep[:, bass.ds(i * GB + u, 1), :]
                                    if kind == "in":
                                        nc.vector.tensor_tensor(slab[:, u, :], g[:, 0:3 * F], b_cat[:], ALU.add)
                                        last = nc.vector.tensor_tensor(own, g[:, 3 * F:4 * F].unsqueeze(1),
                                                                       vec[:, 0, :].unsqueeze(1), ALU.add)
                                    elif kind == "gate":
                                        nc.vector.tensor_copy(slab[:, u, 0:F // 2], g[:, 0:F // 2])
                                        nc.vector.tensor_tensor(slab[:, u, F // 2:F], g[:, F // 2:F],
                                                                b_cat[:, 0:F // 2], ALU.add)
                                        last = nc.vector.tensor_copy(own, g[:, F:2 * F].unsqueeze(1))
                                    elif kind in ("gcn", "mid"):
                                        dcol = dinv[:, bass.ds(i * GB + u + NB, 1)]
                                        nc.vector.tensor_scalar(slab[:, u, 0:F], g[:, 0:F], dcol, None, ALU.mult)
                                        last = nc.vector.tensor_scalar(own, g[:, 0:F].unsqueeze(1), dcol, None, ALU.mult)
                                    else:
                                        last = nc.vector.tensor_copy(slab[:, u, 0:F], g[:, 0:F])
                                    last.then_inc(s_ev, 1)
                                if kind == "gat":
                                    dve.wait_ge(s_ev, i * GB + GB + 2)
                                    for k in range(2):
                                        buf = (tmp, tm2)[k]
                                        last = nc.vector.tensor_tensor(buf[:], slab[:, :, 0:F],
                                                                       over_blocks(vec[:, 2 + k, :]), ALU.mult)
                                        c.link(last)
                                    for k in range(2):
                                        last = nc.vector.tensor_reduce(
                                            er[:, k], (tmp, tm2)[k][:].rearrange("p u (h d) -> p u h d", d=D), AX, ALU.add)
                                    last.then_inc(s_slab, 1)
                                    dve.wait_ge(s_slab, i + 1)
                            assert c.n == steps, (kind, c.n)

        def scale_rows():
            with Phase(nc) as cx:
                s_sc = sem(cx, "sc_scaled")
                s_tb = sem(cx, "sc_stored")
                with nc.Block() as block:
                    @block.vector
                    def _(dve):
                        nc.vector.tensor_tensor(keep[:], keep[:], dinv[:, 0:NB].unsqueeze(2).to_broadcast([P, NB, F]),
                                                ALU.mult).then_inc(s_sc, 1)

                    @block.sync
                    def _(sp):
                        sp.wait_ge(s_sc, 1)
                        sp.dma_start(tab_row[0:NPAD, :].rearrange("(b p) f -> p b f", p=P), keep[:]).then_inc(s_tb, 16)
                        sp.wait_ge(s_tb, 16)

        node_phase("in")
        score_pass(0)
        softmax(0)
        aggregate("sum0", H, False)
        node_phase("gate")
        score_pass(1)
        scale_rows()
        aggregate("sum1", 1, True)
        node_phase("gcn")
        aggregate("sum2", None, True)
        node_phase("mid")
        aggregate("sum3", None, True)
        node_phase("gat")
        score_pass(3)
        softmax(3)
        aggregate("sum4", H, False)
        node_phase("out")


_WEIGHTS = ['L0_gnn_Wq', 'L0_gnn_bq', 'L0_gnn_Wk', 'L0_gnn_bk', 'L0_gnn_Wv', 'L0_gnn_bv', 'L0_gnn_Ws', 'L0_gnn_bs',
            'L0_gnn_Wg', 'L0_gnn_bg', 'L0_gnn_gamma', 'L0_gnn_beta', 'L0_gnn_alpha', 'L1_gnn_mlp_w1', 'L1_gnn_mlp_b1',
            'L1_gnn_mlp_w2', 'L1_gnn_mlp_b2', 'L1_gnn_conv_w', 'L1_gnn_conv_b', 'L2_gnn_W1', 'L2_gnn_b1', 'L2_gnn_W2',
            'L2_gnn_b2', 'L3_gnn_W', 'L3_gnn_a_l', 'L3_gnn_a_r', 'L3_gnn_bias']


def kernel(**inputs):
    import numpy as _np
    import concourse.bacc as _bacc
    from concourse import mybir as _mybir
    from concourse.bass_utils import run_bass_kernel_spmd as _run

    def by_tile(v, fill):
        line = _np.full(EP, fill, v.dtype)
        line[:E] = v
        return _np.ascontiguousarray(line.reshape(T, P).T)

    src, dst = _np.asarray(inputs["src"]), _np.asarray(inputs["dst"])
    line = _np.full((1, EP + 2), N, dst.dtype)
    line[0, 0] = line[0, -1] = -1
    line[0, 1:1 + E] = dst
    arrays = {"x": _np.ascontiguousarray(inputs["x"]), "src_pt": by_tile(src, 0), "dst_pt": by_tile(dst, N),
              "dst_line": line, "ew_pt": by_tile(_np.asarray(inputs["edge_weight"]), 0)}
    for name in _WEIGHTS:
        w = _np.ascontiguousarray(inputs[name])
        arrays[name] = w.reshape(1) if w.ndim == 0 else w
    nc = _bacc.Bacc("TRN2", target_bir_lowering=False, num_devices=1)
    args = {n: nc.dram_tensor("in_" + n, v.shape, _mybir.dt.from_np(v.dtype), kind="ExternalInput").ap()
            for n, v in arrays.items()}
    out = nc.dram_tensor("out_0", (N, F), _mybir.dt.float32, kind="ExternalOutput").ap()
    gnn_kernel(nc, args, out)
    r = _run(nc, [{"in_" + n: v for n, v in arrays.items()}], core_ids=[0])
    return r.results[0]["out_0"]
```

```python
import concourse.bass as bass
from concourse import mybir
from contextlib import ExitStack

fp32 = mybir.dt.float32
i32 = mybir.dt.int32
ALU = mybir.AluOpType
ACT = mybir.ActivationFunctionType
AX = mybir.AxisListType.X

P = 128
N = 6250
E = 106250
F = 128
H = 4
D = F // H
NB = -(-N // P)
NTAIL = N - (NB - 1) * P
NPAD = NB * P
TB = 8
T = -(-E // (P * 32)) * 32
EP = T * P
BATCHES = T // TB
ROUNDS = BATCHES // 2
ROWS = NPAD + P
GB = 7
GROUPS = NB // GB
CH = 32
CT = T // CH
CE = CT * P
BIG = 1e30
SCALE = 1.0 / float(D) ** 0.5
assert NB % GB == 0 and T % CH == 0 and BATCHES % 2 == 0


class Chain:

    def __init__(self, eng, sem, start=0):
        self.eng, self.sem, self.start, self.n = eng, sem, start, 0

    def link(self, ins):
        self.n += 1
        ins.then_inc(self.sem, 1)
        self.eng.wait_ge(self.sem, self.start + self.n)


class Phase(ExitStack):

    def __init__(self, nc):
        super().__init__()
        self.nc, self.sems = nc, []

    def __exit__(self, *exc):
        if self.sems and exc[0] is None:
            self.nc.clear_and_free_semaphores(self.sems)
            self.nc.all_engine_barrier()
        return super().__exit__(*exc)


def gnn_kernel(nc, a, out):
    ctx = ExitStack()

    def sb(name, shape, dt=fp32, where=None):
        return (where or ctx).enter_context(nc.sbuf_tensor(name, shape, dt))

    def ps(where, name, shape):
        return where.enter_context(nc.psum_tensor(name, shape, fp32))

    def sem(where, name):
        s = nc.alloc_semaphore(name)
        where.sems.append(s)
        return s

    def dram(name, shape):
        return nc.dram_tensor(name, shape, fp32, kind="Internal").ap()

    tab_qv = dram("tab_qv", [ROWS, 2 * F])
    tab_k = dram("tab_k", [ROWS, F])
    tab_a = dram("tab_a", [ROWS, F // 2])
    tab_b = dram("tab_b", [ROWS, F // 2])
    tab_row = dram("tab_row", [ROWS, F])
    tab_wh = dram("tab_wh", [ROWS, F + H])
    tab_er = dram("tab_er", [ROWS, H])
    spill = dram("spill", [P, T, F])

    with ctx:
        x_nat = sb("x_nat", [P, NB, F])
        keep = sb("keep", [P, NB, F])
        acc = sb("acc", [P, 2, ROWS])
        score = sb("score", [P, H * T])
        local = sb("local", [P, T + TB])
        src_idx = sb("src_idx", [P, T], i32)
        base = sb("base", [1, T + TB], i32)
        iota = sb("iota", [P, P])
        ident = sb("ident", [P, P])
        dinv = sb("dinv", [P, 2 * NB])
        w_of = {k: sb("w_" + k, [P, n]) for k, n in (("in", 4 * F), ("gate", 2 * F), ("gcn", F), ("mid", F),
                                                     ("gat", F + 2 * H))}
        b_in = sb("b_in", [P, 4 * F])
        b_gate = sb("b_gate", [P, F])
        wg = sb("wg", [P, 3, F])
        wgs = sb("wgs", [P, 2, F])
        att = sb("att", [P, 2 * H])
        gatT = sb("gatT", [P, F])
        ones = sb("ones", [1, 1])
        row_of = {k: sb("r_" + k, [P, F]) for k in ("gamma", "beta", "gcn", "mid", "gat", "out", "mlp")}
        col = sb("col", [P, 3])

        def of_batch(n):
            return score[:].rearrange("p (h t) -> p t h", h=H)[:, bass.ds(n * TB, TB), :]

        def bcast(v, n):
            return bass.AP(tensor=v.tensor, offset=v.offset, ap=[[0, P], [1, n]])

        with Phase(nc) as cx:
            dst_pt = sb("dst_pt", [P, T], i32, cx)
            base_all = sb("base_all", [P, T], i32, cx)
            zero = sb("zero", [P, 2 * F], fp32, cx)
            s_in = sem(cx, "s_in")
            s_zero = sem(cx, "s_zero")
            s_pad = sem(cx, "s_pad")
            s_io = sem(cx, "s_io")
            s_set = sem(cx, "s_set")
            s_ld = sem(cx, "s_ld")
            s_att = sem(cx, "s_att")
            s_gatT = sem(cx, "s_gatT")
            s_gatc = sem(cx, "s_gatc")
            s_wa = sem(cx, "s_wa")
            pW = ps(cx, "pW", [P, 2, F])
            with nc.Block() as block:
                @block.sync
                def _(sp):
                    sp.dma_start(dst_pt[:], a["dst_pt"]).then_inc(s_in, 16)
                    sp.dma_start(base_all[:], bass.AP(tensor=a["dst_pt"].tensor, offset=0, ap=[[0, P], [1, T]])
                                 ).then_inc(s_in, 16)
                    sp.dma_start(src_idx[:], a["src_pt"]).then_inc(s_in, 16)
                    sp.wait_ge(s_zero, 1)
                    sp.dma_start(x_nat[:, 0:NB - 1, :], a["x"][0:(NB - 1) * P, :].rearrange("(b p) f -> p b f", p=P)
                                 ).then_inc(s_in, 16)
                    sp.dma_start(x_nat[0:NTAIL, NB - 1, :], a["x"][(NB - 1) * P:N, :]).then_inc(s_in, 16)
                    loads = [(w_of["in"][:, k * F:(k + 1) * F], a["L0_gnn_W" + c]) for k, c in enumerate("qvks")]
                    loads += [(b_in[:, k * F:(k + 1) * F], bcast(a["L0_gnn_b" + c], F)) for k, c in enumerate("qvks")]
                    loads += [(w_of["gate"][:, 0:F // 2], a["L1_gnn_mlp_w1"][0:F, :]),
                              (w_of["gate"][:, F // 2:F], a["L1_gnn_mlp_w1"][F:2 * F, :]),
                              (w_of["gate"][:, F:2 * F], a["L1_gnn_conv_w"]),
                              (b_gate[:, F // 2:F], bcast(a["L1_gnn_mlp_b1"], F // 2)),
                              (wg[:].rearrange("p k f -> p (k f)"), bcast(a["L0_gnn_Wg"], 3 * F)),
                              (col[:, 0:1], bcast(a["L1_gnn_mlp_b2"], 1)), (col[:, 1:2], bcast(a["L0_gnn_bg"], 1)),
                              (col[:, 2:3], bcast(a["L0_gnn_alpha"], 1)),
                              (row_of["mlp"][:, 0:F // 2], bcast(a["L1_gnn_mlp_w2"], F // 2)),
                              (row_of["gamma"][:], bcast(a["L0_gnn_gamma"], F)),
                              (row_of["beta"][:], bcast(a["L0_gnn_beta"], F)),
                              (w_of["gcn"][:], a["L2_gnn_W1"]), (row_of["gcn"][:], bcast(a["L1_gnn_conv_b"], F)),
                              (w_of["mid"][:], a["L2_gnn_W2"]), (row_of["mid"][:], bcast(a["L2_gnn_b1"], F)),
                              (row_of["gat"][:], bcast(a["L2_gnn_b2"], F)),
                              (row_of["out"][:], bcast(a["L3_gnn_bias"], F))]
                    loads += [(w_of["gat"][:, h * D:(h + 1) * D], a["L3_gnn_W"][h]) for h in range(H)]
                    sp.wait_ge(s_zero, 1)
                    for to, of in loads:
                        sp.dma_start(to, of).then_inc(s_ld, 16)
                    for k, name in enumerate(("L3_gnn_a_l", "L3_gnn_a_r")):
                        for h in range(H):
                            sp.dma_start(att[h * D:(h + 1) * D, k * H + h:k * H + h + 1], a[name][h]).then_inc(s_att, 16)
                    tabs = (tab_qv, tab_k, tab_a, tab_b, tab_row, tab_wh, tab_er)
                    for t in tabs:
                        sp.dma_start(t[NPAD:ROWS, :], zero[:, 0:t.shape[1]]).then_inc(s_pad, 16)
                    sp.wait_ge(s_ld, 16 * len(loads))
                    sp.wait_ge(s_att, 16 * 2 * H)
                    sp.wait_ge(s_pad, 16 * len(tabs))
                    sp.wait_ge(s_in, 16 * 5)

                @block.gpsimd
                def _(pool):
                    nc.gpsimd.iota(iota[:], [[1, P]], base=0, channel_multiplier=0,
                                   allow_small_or_imprecise_dtypes=True).then_inc(s_io, 1)
                    nc.gpsimd.memset(ident[:], 0.0).then_inc(s_io, 1)
                    pool.wait_ge(s_io, 2)
                    nc.gpsimd.affine_select(out=ident[:], in_=ident[:], compare_op=ALU.not_equal, fill=1.0,
                                            base=0, pattern=[[-1, P]], channel_multiplier=1).then_inc(s_io, 1)

                @block.vector
                def _(dve):
                    nc.vector.memset(x_nat[:, NB - 1, :], 0.0)
                    nc.vector.memset(att[:], 0.0)
                    nc.vector.memset(b_gate[:], 0.0)
                    nc.vector.memset(zero[:], 0.0).then_inc(s_zero, 1)
                    nc.vector.memset(local[:], 0.0)
                    nc.vector.memset(base[:], 0)
                    nc.vector.memset(ones[:], 1.0).then_inc(s_set, 1)
                    dve.wait_ge(s_in, 16 * 5)
                    dve.wait_ge(s_set, 1)
                    nc.vector.tensor_tensor(local[:, 0:T], dst_pt[:], base_all[:], ALU.subtract)
                    nc.vector.tensor_copy(base[0:1, 0:T], dst_pt[0:1, :])
                    dve.wait_ge(s_ld, 16 * 29)
                    nc.vector.tensor_tensor(wgs[:, 0, :], wg[:, 0, :], wg[:, 2, :], ALU.add)
                    nc.vector.tensor_tensor(wgs[:, 1, :], wg[:, 1, :], wg[:, 2, :], ALU.subtract)
                    dve.wait_ge(s_gatT, 1)
                    nc.vector.tensor_copy(gatT[:], pW[:, 0, :]).then_inc(s_gatc, 1)
                    dve.wait_ge(s_wa, 1)
                    nc.vector.tensor_copy(w_of["gat"][:, F:F + 2 * H], pW[:, 1, 0:2 * H])

                @block.tensor
                def _(pe):
                    pe.wait_ge(s_ld, 16 * 29)
                    pe.wait_ge(s_io, 3)
                    nc.tensor.transpose(pW[:, 0, :], w_of["gat"][:, 0:F], ident[:]).then_inc(s_gatT, 1)
                    pe.wait_ge(s_gatc, 1)
                    pe.wait_ge(s_att, 16 * 2 * H)
                    nc.tensor.matmul(pW[:, 1, 0:2 * H], gatT[:], att[:], start=True, stop=True).then_inc(s_wa, 1)

        def onehot(dst, n):
            return nc.vector.tensor_tensor(dst, iota[:].unsqueeze(1).to_broadcast([P, TB, P]),
                                           local[:, bass.ds(n * TB, TB)].unsqueeze(2).to_broadcast([P, TB, P]),
                                           ALU.is_equal)

        def score_pass(layer):
            table, win = {0: (tab_qv, tab_k), 1: (tab_a, tab_b), 3: (tab_wh, tab_er)}[layer]
            RW, WW = table.shape[1], win.shape[1]
            spills = layer != 1
            v0 = F if layer == 0 else 0
            with Phase(nc) as cx:
                L = f"l{layer}_"
                idx = sb(L + "idx", [P, 2 * TB], i32, cx)
                rows = sb(L + "rows", [P, 2 * TB, RW], fp32, cx)
                hot = sb(L + "hot", [P, 2, TB, P], fp32, cx)
                hotT = sb(L + "hotT", [P, 2, TB, P], fp32, cx)
                winr = sb(L + "winr", [P, 2 * TB, WW], fp32, cx)
                pT = ps(cx, L + "pT", [P, TB, P])
                pK = ps(cx, L + "pK", [P, 2, TB, max(WW, F // 2)])[:, :, :, 0:WW]
                s_rows = [sem(cx, L + f"s_rows{b}") for b in range(2)]
                s_win = [sem(cx, L + f"s_win{b}") for b in range(2)]
                s_spill = [sem(cx, L + f"s_spill{b}") for b in range(2)]
                s_idx = sem(cx, L + "s_idx")
                s_used = sem(cx, L + "s_used")
                s_hot = sem(cx, L + "s_hot")
                s_tr = sem(cx, L + "s_tr")
                s_hotT = sem(cx, L + "s_hotT")
                s_dst = sem(cx, L + "s_dst")
                s_chain = sem(cx, L + "s_chain")
                s_ew = sem(cx, L + "s_ew")
                if layer == 1:
                    pre = sb(L + "pre", [P, 2, TB, WW], fp32, cx)
                    act = sb(L + "act", [P, 2, TB, WW], fp32, cx)
                    logit = sb(L + "logit", [P, 2, TB], fp32, cx)
                    lo = sb(L + "lo", [P, 2, TB, P], fp32, cx)
                    hi = sb(L + "hi", [P, 2, TB, 2 * NB], fp32, cx)
                    dst_i = sb(L + "dst_i", [P, T], i32, cx)
                    dst_d = sb(L + "dst_d", [P, T], i32, cx)
                    dlo, dhi = acc[:, 0, 0:T], acc[:, 1, 0:T]
                    zer = sb(L + "zer", [P, P], fp32, cx)
                    pD = ps(cx, L + "pD", [P, 2 * NB])
                    s_dl = sem(cx, L + "s_dl")
                    s_pre = s_used
                    s_act = sem(cx, L + "s_act")
                    s_logit = sem(cx, L + "s_logit")
                    s_edge = sem(cx, L + "s_edge")
                    s_hi = sem(cx, L + "s_hi")
                    s_count = sem(cx, L + "s_count")
                    s_deg = sem(cx, L + "s_deg")
                    s_dend = sem(cx, L + "s_dend")
                    s_sqrt = sem(cx, L + "s_sqrt")
                    s_zer = sem(cx, L + "s_zer")
                if layer == 0:
                    prod = sb(L + "prod", [P, 2, TB, F], fp32, cx)
                if layer == 3:
                    lin = sb(L + "lin", [P, 2, TB, H], fp32, cx)
                    lnw = sb(L + "lnw", [P, T], fp32, cx)
                    s_lin = sem(cx, L + "s_lin")
                    s_lnc = sem(cx, L + "s_lnc")
                    s_lnw = sem(cx, L + "s_lnw")

                with nc.Block() as block:
                    @block.sync
                    def _(sp):
                        if layer == 1:
                            sp.dma_start(dst_i[:], a["dst_pt"]).then_inc(s_dl, 16)
                            sp.sem_inc(s_deg, 2)
                        if layer == 3:
                            sp.dma_start(lnw[:], a["ew_pt"]).then_inc(s_ew, 16)
                        sp.sem_inc(s_dst, 2)
                        for b in range(2):
                            sp.sem_inc(s_spill[b], 16)
                        regs = [sp.alloc_register(L + f"win{u}") for u in range(TB)]

                        def load_windows(n, b):
                            sp.load(regs, base[0:1, bass.ds(n * TB, TB)])
                            sp.wait_ge(s_dst, n + 1)
                            for u in range(TB):
                                at = sp.snap(regs[u], min_val=0, max_val=N)
                                sp.dma_start(winr[:, b * TB + u, :], win[bass.ds(at, P), :]).then_inc(s_win[b], 16)

                        def store_values(n, b, i):
                            sp.wait_ge(s_rows[b], i * (16 * TB) + 16 * TB)
                            sp.dma_start(spill[:, bass.ds(n * TB, TB), :], rows[:, b * TB:(b + 1) * TB, v0:v0 + F]
                                         ).then_inc(s_spill[b], 16)

                        load_windows(0, 0)
                        with sp.Fori(0, ROUNDS) as i:
                            for b in range(2):
                                load_windows(i * 2 + b + 1, 1 - b)
                                if spills:
                                    store_values(i * 2 + b, b, i)
                        if spills:
                            for b in range(2):
                                sp.wait_ge(s_spill[b], 16 * (ROUNDS + 1))
                        sp.wait_ge(s_win[0], 16 * TB * (ROUNDS + 1))

                    @block.gpsimd
                    def _(pool):
                        pool.sem_inc(s_used, 2)
                        with pool.Fori(0, ROUNDS) as i:
                            for b in range(2):
                                pool.wait_ge(s_used, i * 2 + b + 1)
                                if spills:
                                    pool.wait_ge(s_spill[b], i * 16 + 16)
                                nc.gpsimd.tensor_copy(idx[:, b * TB:(b + 1) * TB],
                                                      src_idx[:, bass.ds((i * 2 + b) * TB, TB)]).then_inc(s_idx, 1)
                                pool.wait_ge(s_idx, 1)
                                pool.wait_ge(s_idx, i * 2 + b + 1)
                                for u in range(b * TB, (b + 1) * TB):
                                    nc.gpsimd.indirect_dma_start(
                                        rows[:, u, :], None, table,
                                        bass.IndirectOffsetOnAxis(idx[:, u:u + 1], 0)).then_inc(s_rows[b], 16)

                    @block.tensor
                    def _(pe):
                        def turn(n, b):
                            pe.wait_ge(s_hot, n + 1)
                            for u in range(TB):
                                last = nc.tensor.transpose(pT[:, u, :], hot[:, b, u, :], ident[:])
                            last.then_inc(s_tr, 1)

                        if layer == 1:
                            pe.wait_ge(s_zer, 1)
                            nc.tensor.matmul(pD[:], zer[:], zer[:, 0:2 * NB], start=True, stop=False)
                        def spread(n, b, i):
                            pe.wait_ge(s_win[b], i * (16 * TB) + 16 * TB)
                            pe.wait_ge(s_used, n + 1)
                            for u in range(TB):
                                last = nc.tensor.matmul(pK[:, b, u, :], hotT[:, b, u, :], winr[:, b * TB + u, :],
                                                        start=True, stop=True)
                            last.then_inc(s_dst, 1)

                        def degrees(n, b):
                            pe.wait_ge(s_hi, n + 1)
                            for u in range(TB):
                                last = nc.tensor.matmul(pD[:], lo[:, b, u, :], hi[:, b, u, :], start=False, stop=False)
                            last.then_inc(s_deg, 1)

                        def step(n, b, i):
                            pe.wait_ge(s_hotT, n + 1)
                            spread(n, b, i)
                            turn(n + 1, 1 - b)

                        turn(0, 0)
                        step(0, 0, 0)
                        step(1, 1, 0)
                        with pe.Fori(0, ROUNDS - 1) as i:
                            for b in range(2):
                                step(i * 2 + b + 2, b, i + 1)
                                if layer == 1:
                                    degrees(i * 2 + b, b)
                        if layer == 1:
                            degrees(BATCHES - 2, 0)
                            degrees(BATCHES - 1, 1)
                            nc.tensor.matmul(pD[:], zer[:], zer[:, 0:2 * NB], start=False, stop=True
                                             ).then_inc(s_dend, 1)

                    @block.scalar
                    def _(act_e):
                        def copy_turned(n, b):
                            act_e.wait_ge(s_tr, n + 2)
                            act_e.wait_ge(s_dst, n + 1)
                            nc.scalar.activation(hotT[:, b, 0:4, :], pT[:, 0:4, :], ACT.Copy)
                            nc.scalar.activation(hotT[:, b, 4:8, :], pT[:, 4:8, :], ACT.Copy).then_inc(s_hotT, 1)

                        if layer == 3:
                            act_e.wait_ge(s_lnc, 1)
                            nc.scalar.activation(lnw[:], lnw[:], ACT.Ln).then_inc(s_lnw, 1)
                        copy_turned(0, 0)
                        with act_e.Fori(0, ROUNDS) as i:
                            for b in range(2):
                                n = i * 2 + b
                                if layer == 1:
                                    act_e.wait_ge(s_pre, n + 3)
                                    nc.scalar.activation(act[:, b], pre[:, b], ACT.Gelu).then_inc(s_act, 1)
                                copy_turned(n + 1, 1 - b)
                                if layer == 1:
                                    act_e.wait_ge(s_logit, n + 1)
                                    nc.scalar.activation(score[:, bass.ds(n * TB, TB)], logit[:, b], ACT.Sigmoid,
                                                         bias=col[:, 0:1]).then_inc(s_edge, 1)
                        if layer == 1:
                            act_e.wait_ge(s_dend, 2)
                            nc.scalar.activation(dinv[:], dinv[:], ACT.Sqrt).then_inc(s_sqrt, 1)

                    @block.vector
                    def _(dve):
                        if layer == 1:
                            nc.vector.memset(zer[:], 0.0).then_inc(s_zer, 1)
                            dve.wait_ge(s_dl, 16)
                            pc = Chain(dve, s_ew)
                            pc.link(nc.vector.tensor_scalar(dst_d[:], dst_i[:], P - 1, None, ALU.bitwise_and))
                            pc.link(nc.vector.tensor_copy(dlo, dst_d[:]))
                            pc.link(nc.vector.tensor_scalar(dst_d[:], dst_i[:], 7, None, ALU.logical_shift_right))
                            pc.link(nc.vector.tensor_copy(dhi, dst_d[:]))
                        if layer == 3:
                            dve.wait_ge(s_ew, 16)
                            nc.vector.tensor_scalar(lnw[:], lnw[:], 1e-8, None, ALU.max).then_inc(s_lnc, 1)
                            dve.wait_ge(s_lnw, 1)
                        dve.sem_inc(s_tr, 1)
                        onehot(hot[:, 0], 0).then_inc(s_hot, 1)

                        def meet(n, b, i):
                            rb = rows[:, b * TB:(b + 1) * TB, :]
                            dve.wait_ge(s_tr, n + 1)
                            onehot(hot[:, 1 - b], n + 1).then_inc(s_hot, 1)
                            dve.wait_ge(s_dst, n + 3)
                            dve.wait_ge(s_rows[b], i * (16 * TB) + 16 * TB)
                            if layer == 0:
                                for g in range(2):
                                    nc.vector.tensor_tensor(prod[:, b, 4 * g:4 * g + 4, :], rb[:, 4 * g:4 * g + 4, 0:F],
                                                            pK[:, b, 4 * g:4 * g + 4, :], ALU.mult).then_inc(s_chain, 1)
                                dve.wait_ge(s_chain, 2)
                                dve.wait_ge(s_chain, n * 2 + 2)
                                nc.vector.tensor_reduce(
                                    of_batch(n), prod[:, b].rearrange("p t (h d) -> p t h d", d=D), AX, ALU.add
                                ).then_inc(s_used, 1)
                            if layer == 1:
                                nc.vector.tensor_tensor(pre[:, b], rb, pK[:, b], ALU.add).then_inc(s_pre, 1)
                            if layer == 3:
                                nc.vector.tensor_tensor(lin[:, b], rb[:, :, F:F + H], pK[:, b], ALU.add
                                                        ).then_inc(s_chain, 1)
                                dve.wait_ge(s_chain, n * 2 + 1)
                                nc.vector.scalar_tensor_tensor(lin[:, b], lin[:, b], 0.2, lin[:, b],
                                                               ALU.mult, ALU.max).then_inc(s_chain, 1)
                                dve.wait_ge(s_chain, n * 2 + 2)
                                nc.vector.tensor_tensor(
                                    of_batch(n), lin[:, b],
                                    lnw[:, bass.ds(n * TB, TB)].unsqueeze(2).to_broadcast([P, TB, H]), ALU.add
                                ).then_inc(s_used, 1)

                        def mlp_out(n, b):
                            dve.wait_ge(s_act, n + 1)
                            nc.vector.tensor_tensor(act[:, b], act[:, b],
                                                    row_of["mlp"][:, 0:WW].unsqueeze(1).to_broadcast([P, TB, WW]), ALU.mult
                                                    ).then_inc(s_chain, 1)
                            dve.wait_ge(s_chain, n + 1)
                            nc.vector.tensor_reduce(logit[:, b], act[:, b], AX, ALU.add).then_inc(s_logit, 1)

                        def degree_operands(n, b):
                            dve.wait_ge(s_deg, n + 1)
                            nc.vector.tensor_tensor(
                                lo[:, b], iota[:].unsqueeze(1).to_broadcast([P, TB, P]),
                                dlo[:, bass.ds(n * TB, TB)].unsqueeze(2).to_broadcast([P, TB, P]), ALU.is_equal)
                            nc.vector.tensor_tensor(
                                hi[:, b, :, NB:2 * NB], iota[:, 0:NB].unsqueeze(1).to_broadcast([P, TB, NB]),
                                dhi[:, bass.ds(n * TB, TB)].unsqueeze(2).to_broadcast([P, TB, NB]),
                                ALU.is_equal).then_inc(s_count, 1)
                            dve.wait_ge(s_edge, n + 1)
                            dve.wait_ge(s_count, n + 1)
                            nc.vector.tensor_tensor(
                                hi[:, b, :, 0:NB], hi[:, b, :, NB:2 * NB],
                                score[:, bass.ds(n * TB, TB)].unsqueeze(2).to_broadcast([P, TB, NB]),
                                ALU.mult).then_inc(s_hi, 1)

                        if layer == 1:
                            meet(0, 0, 0)
                            mlp_out(0, 0)
                            with dve.Fori(0, ROUNDS - 1) as i:
                                meet(i * 2 + 1, 1, i)
                                degree_operands(i * 2, 0)
                                mlp_out(i * 2 + 1, 1)
                                meet(i * 2 + 2, 0, i + 1)
                                degree_operands(i * 2 + 1, 1)
                                mlp_out(i * 2 + 2, 0)
                            meet(BATCHES - 1, 1, ROUNDS - 1)
                            degree_operands(BATCHES - 2, 0)
                            mlp_out(BATCHES - 1, 1)
                            degree_operands(BATCHES - 1, 1)
                        else:
                            with dve.Fori(0, ROUNDS) as i:
                                for b in range(2):
                                    meet(i * 2 + b, b, i)
                        if layer == 1:
                            dve.wait_ge(s_dend, 1)
                            nc.vector.tensor_scalar(dinv[:], pD[:], 1.0, None, ALU.add).then_inc(s_dend, 1)
                            dve.wait_ge(s_sqrt, 1)
                            nc.vector.reciprocal(dinv[:], dinv[:])

        def softmax(layer):
            scale, eps = (SCALE, 0.0) if layer == 0 else (1.0, 1e-8)
            with Phase(nc) as cx:
                L = f"x{layer}_"
                dchunk = sb(L + "dchunk", [P, CE + 2], i32, cx)
                room = acc[:].rearrange("p k n -> p (k n)")
                same = room[:, 0:CE + 1]
                brk = room[:, CE + 1:2 * CE + 2]
                lg = sb(L + "lg", [P, CE], fp32, cx)
                fw = room[:, 2 * CE + 2:3 * CE + 2]
                bw = sb(L + "bw", [P, CE], fp32, cx)
                whole = sb(L + "whole", [P, 2], fp32, cx)
                rowg = sb(L + "rowg", [1, 2, P], fp32, cx)
                rowp = sb(L + "rowp", [1, 2, P], fp32, cx)
                carry = sb(L + "carry", [1, 4, P + 1], fp32, cx)
                init = sb(L + "init", [P, 4], fp32, cx)
                pB = ps(cx, L + "pB", [P, CT, P])
                pR = ps(cx, L + "pR", [P, 4 * P])
                s_dc = sem(cx, L + "s_dc")
                s_turn = sem(cx, L + "s_turn")
                s_lg = sem(cx, L + "s_lg")
                s_whole = sem(cx, L + "s_whole")
                s_rowg = sem(cx, L + "s_rowg")
                s_end = sem(cx, L + "s_end")
                s_row = sem(cx, L + "s_row")
                s_car = sem(cx, L + "s_car")
                s_init = sem(cx, L + "s_init")
                s_c = sem(cx, L + "s_c")
                s_exp = sem(cx, L + "s_exp")
                s_diff = sem(cx, L + "s_diff")
                s_w = sem(cx, L + "s_w")
                s_back = sem(cx, L + "s_back")
                by_chunk = score[:].rearrange("p (q j) -> p j q", j=CT)
                ends = [(fw, CE - 1), (bw, 0), (fw, CE - 1), (bw, 0)]
                with nc.Block() as block:
                    @block.sync
                    def _(sp):
                        for h in range(H):
                            sp.dma_start(dchunk[h * CH:(h + 1) * CH, :],
                                         bass.AP(tensor=a["dst_line"].tensor, offset=0, ap=[[CE, CH], [1, CE + 2]])
                                         ).then_inc(s_dc, 16)
                        sp.wait_ge(s_dc, 16 * H)

                    @block.tensor
                    def _(pe):
                        for j in range(CT):
                            last = nc.tensor.transpose(pB[:, j, :], by_chunk[:, j], ident[:])
                        last.then_inc(s_turn, 1)
                        pe.wait_ge(s_whole, 1)
                        for k in range(2):
                            last = nc.tensor.matmul(pR[0:1, k * P:(k + 1) * P], whole[:, k:k + 1], ident[:],
                                                    start=True, stop=True)
                        last.then_inc(s_rowg, 1)
                        for k, (buf, at) in enumerate(ends):
                            pe.wait_ge(s_end, k + 1)
                            nc.tensor.matmul(pR[0:1, 2 * P:3 * P], buf[:, at:at + 1], ident[:], start=True, stop=True
                                             ).then_inc(s_row, 1)
                            pe.wait_ge(s_car, k + 1)
                            o = k % 2
                            nc.tensor.matmul(pR[:, 3 * P:3 * P + 1], carry[0:1, k, o:o + P], ones[:],
                                             start=True, stop=True).then_inc(s_init, 1)
                        pe.wait_ge(s_w, 1)
                        for j in range(CT):
                            last = nc.tensor.transpose(pB[:, j, :], lg[:, j * P:(j + 1) * P], ident[:])
                        last.then_inc(s_back, 1)

                    @block.scalar
                    def _(act_e):
                        act_e.wait_ge(s_turn, 1)
                        for j in range(0, CT, 4):
                            m = min(4, CT - j)
                            last = nc.scalar.activation(lg[:, j * P:(j + m) * P].rearrange("p (j e) -> p j e", e=P),
                                                        pB[:, j:j + m, :], ACT.Copy)
                        last.then_inc(s_lg, 1)
                        act_e.wait_ge(s_diff, 1)
                        nc.scalar.activation(lg[:], lg[:], ACT.Exp, scale=scale).then_inc(s_exp, 1)
                        act_e.wait_ge(s_back, 1)
                        for j in range(0, CT, 4):
                            m = min(4, CT - j)
                            nc.scalar.activation(by_chunk[:, j:j + m], pB[:, j:j + m, :], ACT.Copy)

                    @block.vector
                    def _(dve):
                        c = Chain(dve, s_c)
                        dve.wait_ge(s_dc, 16 * H)
                        c.link(nc.vector.tensor_tensor(same, dchunk[:, 0:CE + 1], dchunk[:, 1:CE + 2], ALU.is_equal))
                        nc.vector.tensor_reduce(whole[:, 0:1], same[:, 0:CE], AX, ALU.min)
                        nc.vector.tensor_reduce(whole[:, 1:2], same[:, 1:CE + 1], AX, ALU.min).then_inc(s_whole, 1)
                        nc.vector.tensor_scalar(brk, same, 1.0, BIG, ALU.subtract, ALU.mult)
                        nc.vector.memset(carry[:], -BIG)
                        dve.wait_ge(s_rowg, 1)
                        c.link(nc.vector.tensor_copy(rowg[:].rearrange("p k n -> p (k n)"), pR[0:1, 0:2 * P]))
                        c.link(nc.vector.tensor_scalar(rowp[:], rowg[:], 1.0, BIG, ALU.subtract, ALU.mult))
                        c.link(nc.vector.memset(carry[:, 2, :], 0.0))

                        def segment_scan(k, out, data, marks, rows_, op0, op1, start):
                            back = k % 2
                            m = marks[:, 1:CE + 1] if back else marks[:, 0:CE]
                            rev = (lambda ap: ap[:, ::-1]) if back else (lambda ap: ap)
                            nc.vector.tensor_tensor_scan(rev(out), rev(m), rev(data), start, op0, op1
                                                         ).then_inc(s_end, 1)
                            dve.wait_ge(s_row, k + 1)
                            row = pR[0:1, 2 * P:3 * P]
                            to = carry[:, k, 0:P] if back else carry[:, k, 1:P + 1]
                            nc.vector.tensor_tensor_scan(rev(to), rev(rows_[:, back, :]), rev(row), start, op0, op1
                                                         ).then_inc(s_car, 1)
                            dve.wait_ge(s_init, k + 1)
                            c.link(nc.vector.tensor_copy(init[:, k:k + 1], pR[:, 3 * P:3 * P + 1]))
                            c.link(nc.vector.tensor_tensor_scan(rev(out), rev(m), rev(data), init[:, k:k + 1],
                                                                op0, op1))

                        dve.wait_ge(s_lg, 1)
                        segment_scan(0, fw, lg[:], brk, rowp, ALU.add, ALU.max, -BIG)
                        segment_scan(1, bw[:], fw, brk, rowp, ALU.add, ALU.max, -BIG)
                        nc.vector.tensor_tensor(lg[:], lg[:], bw[:], ALU.subtract).then_inc(s_diff, 1)
                        dve.wait_ge(s_exp, 1)
                        segment_scan(2, fw, lg[:], same, rowg, ALU.mult, ALU.add, 0.0)
                        segment_scan(3, bw[:], fw, brk, rowp, ALU.add, ALU.max, -BIG)
                        if eps:
                            c.link(nc.vector.tensor_scalar(bw[:], bw[:], eps, None, ALU.add))
                        c.link(nc.vector.reciprocal(bw[:], bw[:]))
                        nc.vector.tensor_tensor(lg[:], lg[:], bw[:], ALU.mult).then_inc(s_w, 1)

        def aggregate(name, weights, gather):
            with Phase(nc) as cx:
                L = name + "_"
                hot = sb(L + "hot", [P, 2, TB, P], fp32, cx)
                rows = sb(L + "rows", [P, 2 * TB, F], fp32, cx)
                idx = sb(L + "idx", [P, 2 * TB], i32, cx)
                wrow = sb(L + "wrow", [P, 2 * TB, F], fp32, cx) if weights else rows
                pA = ps(cx, L + "pA", [P, 2, TB, P])
                s_rows = [sem(cx, L + f"s_rows{b}") for b in range(2)]
                s_idx = sem(cx, L + "s_idx")
                s_hot = sem(cx, L + "s_hot")
                s_wrow = sem(cx, L + "s_wrow")
                s_sum = sem(cx, L + "s_sum")
                s_free = s_wrow if weights else s_sum
                s_add = sem(cx, L + "s_add")
                def weigh(eng, n, b):
                    half = slice(b * TB, (b + 1) * TB)
                    if weights == H:
                        return eng.tensor_tensor(wrow[:, half, :].rearrange("p t (h d) -> p t h d", d=D),
                                                 rows[:, half, :].rearrange("p t (h d) -> p t h d", d=D),
                                                 of_batch(n).unsqueeze(3).to_broadcast([P, TB, H, D]), ALU.mult)
                    return eng.tensor_tensor(wrow[:, half, :], rows[:, half, :],
                                             score[:, bass.ds(n * TB, TB)].unsqueeze(2).to_broadcast([P, TB, F]),
                                             ALU.mult)

                with nc.Block() as block:
                    @block.gpsimd
                    def _(pool):
                        pool.sem_inc(s_wrow, 2)
                        if not gather:
                            with pool.Fori(0, ROUNDS) as i:
                                for b in range(2):
                                    pool.wait_ge(s_sum, i * 2 + b + 1)
                                    pool.wait_ge(s_rows[b], 16)
                                    pool.wait_ge(s_rows[b], i * 16 + 16)
                                    weigh(nc.gpsimd, i * 2 + b, b).then_inc(s_wrow, 1)
                        if gather:
                            with pool.Fori(0, ROUNDS) as i:
                                for b in range(2):
                                    pool.wait_ge(s_free, i * 2 + b + 1)
                                    nc.gpsimd.tensor_copy(idx[:, b * TB:(b + 1) * TB],
                                                          src_idx[:, bass.ds((i * 2 + b) * TB, TB)]).then_inc(s_idx, 1)
                                    pool.wait_ge(s_idx, 1)
                                    pool.wait_ge(s_idx, i * 2 + b + 1)
                                    for u in range(b * TB, (b + 1) * TB):
                                        nc.gpsimd.indirect_dma_start(
                                            rows[:, u, :], None, tab_row,
                                            bass.IndirectOffsetOnAxis(idx[:, u:u + 1], 0)).then_inc(s_rows[b], 16)

                    @block.sync
                    def _(sp):
                        if not gather:
                            with sp.Fori(0, ROUNDS) as i:
                                for b in range(2):
                                    sp.wait_ge(s_free, i * 2 + b + 1)
                                    sp.dma_start(rows[:, b * TB:(b + 1) * TB, :],
                                                 spill[:, bass.ds((i * 2 + b) * TB, TB), :]).then_inc(s_rows[b], 16)

                    per_batch = 16 * TB if gather else 16

                    @block.tensor
                    def _(pe):
                        with pe.Fori(0, ROUNDS) as i:
                            for b in range(2):
                                n = i * 2 + b
                                pe.wait_ge(s_hot, n + 1)
                                if weights:
                                    pe.wait_ge(s_wrow, n + 3)
                                else:
                                    pe.wait_ge(s_rows[b], i * per_batch + per_batch)
                                for u in range(TB):
                                    last = nc.tensor.matmul(pA[:, b, u, :], wrow[:, b * TB + u, :], hot[:, b, u, :],
                                                            start=True, stop=True)
                                last.then_inc(s_sum, 1)

                    @block.vector
                    def _(dve):
                        regs = [dve.alloc_register(L + f"at{u}") for u in range(TB)]

                        def prepare(n, b, i):
                            dve.wait_ge(s_sum, n + 1)
                            onehot(hot[:, b], n).then_inc(s_hot, 1)
                            if weights and gather:
                                dve.wait_ge(s_rows[b], i * per_batch + per_batch)
                                weigh(nc.vector, n, b).then_inc(s_wrow, 1)

                        def add_windows(n, b):
                            dve.load(regs, base[0:1, bass.ds(n * TB, TB)])
                            dve.wait_ge(s_sum, n + 3)
                            for u in range(TB):
                                at = dve.snap(regs[u], min_val=0, max_val=N)
                                dve.wait_ge(s_add, n * TB + u + 1)
                                nc.vector.tensor_tensor(acc[:, u % 2, bass.ds(at, P)], acc[:, u % 2, bass.ds(at, P)],
                                                        pA[:, b, u, :], ALU.add).then_inc(s_add, 1)

                        dve.sem_inc(s_sum, 2)
                        nc.vector.memset(acc[:], 0.0).then_inc(s_add, 2)
                        prepare(0, 0, 0)
                        with dve.Fori(0, ROUNDS - 1) as i:
                            prepare(i * 2 + 1, 1, i)
                            add_windows(i * 2, 0)
                            prepare(i * 2 + 2, 0, i + 1)
                            add_windows(i * 2 + 1, 1)
                        prepare(BATCHES - 1, 1, ROUNDS - 1)
                        add_windows(BATCHES - 2, 0)
                        add_windows(BATCHES - 1, 1)

        def node_phase(kind):
            cols = w_of[kind].shape[1] if kind in w_of else 0
            sums = kind != "in"
            own = {"gcn": keep, "mid": keep, "gat": keep, "out": x_nat}.get(kind)
            norms = {"gate": 2, "mid": 0, "out": 0}.get(kind, 1)
            slabbed = kind in ("in", "gate", "gat")
            SW = {"in": 3 * F, "gate": F, "gat": F + 2 * H}.get(kind, 1)
            RING = 4
            with Phase(nc) as cx:
                L = kind + "_"
                xin = sb(L + "xin", [P, 2, GB, F], fp32, cx)
                hb = sb(L + "hb", [P, 2, GB, F], fp32, cx)
                tmp = sb(L + "tmp", [P, GB, F], fp32, cx)
                tm2 = sb(L + "tm2", [P, GB, F], fp32, cx)
                gskip = sb(L + "gskip", [P, 2, GB, F], fp32, cx) if kind == "gate" else None
                accs = sb(L + "accs", [P, 2, GB * P], fp32, cx)
                hT = sb(L + "hT", [P, GB * P], fp32, cx)
                stats = sb(L + "stats", [P, GB, 6], fp32, cx)
                mv = sb(L + "mv", [P, GB, 2], fp32, cx)
                rss = sb(L + "rss", [P, 2, 2, GB], fp32, cx)
                nbs = sb(L + "nbs", [P, 2, 2, GB], fp32, cx)
                spacer = sb(L + "spacer", [P, 1], fp32, cx)
                z = sb(L + "z", [P, 2, GB], fp32, cx)
                slab = sb(L + "slab", [P, 2, GB, SW], fp32, cx)
                pA = ps(cx, L + "pA", [P, 8, P])
                pH = ps(cx, L + "pH", [P, 8, P])
                pG = ps(cx, L + "pG", [P, RING, 4 * F])
                s_c = sem(cx, L + "s_c")
                s_stage = sem(cx, L + "s_stage")
                s_sums = sem(cx, L + "s_sums")
                s_read = sem(cx, L + "s_read")
                s_var = sem(cx, L + "s_var")
                s_std = sem(cx, L + "s_std")
                s_nb = sem(cx, L + "s_nb")
                s_n1 = sem(cx, L + "s_n1")
                s_z = sem(cx, L + "s_z")
                s_gate = sem(cx, L + "s_gate")
                s_skip = sem(cx, L + "s_skip")
                s_h = sem(cx, L + "s_h")
                s_ht = sem(cx, L + "s_ht")
                s_hT = sem(cx, L + "s_hT")
                s_mm = sem(cx, L + "s_mm")
                s_ev = sem(cx, L + "s_ev")
                s_st = [sem(cx, L + f"s_st{b}") for b in range(2)]
                s_x = sem(cx, L + "s_x")

                def rows_of(table, g, c0, c1):
                    return table[0:NPAD, c0:c1].rearrange("(b p) c -> p b c", p=P)[:, bass.ds(g * GB, GB), :]

                stores = {"in": [(tab_qv, 0, 2 * F, 0), (tab_k, 0, F, 2 * F)],
                          "gate": [(tab_a, 0, F // 2, 0), (tab_b, 0, F // 2, F // 2)],
                          "gcn": [(tab_row, 0, F, 0)], "mid": [(tab_row, 0, F, 0)],
                          "gat": [(tab_wh, 0, F + H, 0), (tab_er, 0, H, F + H)], "out": []}[kind]

                def groups(eng, body):
                    with eng.Fori(0, (GROUPS - 3) // 2) as i:
                        for b in range(2):
                            body(i * 2 + b, b, i)
                    for g in range(GROUPS - 3, GROUPS):
                        body(g, g % 2, g // 2)

                def there(g, n=0):
                    return not isinstance(g, int) or g + n < GROUPS

                assert GROUPS % 2 == 1
                with nc.Block() as block:
                    @block.sync
                    def _(sp):
                        sp.sem_inc(s_st[0], 16)
                        sp.sem_inc(s_st[1], 16)
                        sp.sem_inc(s_ht, 2)
                        sp.sem_inc(s_hT, 1)
                        sp.sem_inc(s_mm, GB)
                        sp.sem_inc(s_sums, 1)
                        sp.sem_inc(s_read, 1)
                        sp.sem_inc(s_ev, RING)

                        def store(g, b, i):
                            if kind == "out":
                                sp.wait_ge(s_x, g + 1)
                                if there(g, 1):
                                    sp.dma_start(out[0:(NB - 1) * P, :].rearrange("(b p) f -> p b f", p=P)
                                                 [:, bass.ds(g * GB, GB), :],
                                                 x_nat[:, bass.ds(g * GB, GB), :]).then_inc(s_st[b], 16)
                                else:
                                    sp.dma_start(out[g * GB * P:(NB - 1) * P, :].rearrange("(b p) f -> p b f", p=P),
                                                 x_nat[:, g * GB:NB - 1, :]).then_inc(s_st[b], 16)
                                    sp.dma_start(out[(NB - 1) * P:N, :], x_nat[0:NTAIL, NB - 1, :]
                                                 ).then_inc(s_st[1 - b], 16)
                                return
                            sp.wait_ge(s_ev, g * GB + GB + RING)
                            for table, c0, c1, at in stores:
                                of = slab[:, b, :, at:at + c1 - c0] if slabbed else keep[:, bass.ds(g * GB, GB), :]
                                sp.dma_start(rows_of(table, g, c0, c1), of).then_inc(s_st[b], 16)

                        groups(sp, store)
                        m = max(len(stores), 1)
                        sp.wait_ge(s_st[0], 16 + 16 * m * (GROUPS + 1) // 2)
                        sp.wait_ge(s_st[1], 16 + 16 * m * (GROUPS // 2) + (16 if kind == "out" else 0))

                    @block.gpsimd
                    def _(pool):
                        if kind == "gate":
                            def skip_part(g, b, i):
                                pool.wait_ge(s_read, 1)
                                pool.wait_ge(s_read, g + 1)
                                nc.gpsimd.tensor_tensor(gskip[:, b], keep[:, bass.ds(g * GB, GB), :],
                                                        wgs[:, 0, :].unsqueeze(1).to_broadcast([P, GB, F]), ALU.mult
                                                        ).then_inc(s_skip, 1)
                            groups(pool, skip_part)

                    @block.scalar
                    def _(ae):
                        def stage(g):
                            if sums:
                                ae.wait_ge(s_sums, g + 1)
                                nc.scalar.activation(accs[:], acc[:, :, bass.ds(g * (GB * P), GB * P)], ACT.Copy
                                                     ).then_inc(s_stage, 1)

                        def normalise(to, of, k, which, func):
                            b, m = which
                            rs, nb = rss[:, b, m], nbs[:, b, m]
                            ae.wait_ge(s_var, k)
                            nc.scalar.activation(rs, rs, ACT.Sqrt).then_inc(s_std, 1)
                            ae.wait_ge(s_nb, k)
                            for u in range(GB):
                                last = nc.scalar.activation(to[:, u, :], of[:, u, :], func, scale=rs[:, u:u + 1],
                                                            bias=nb[:, u:u + 1])
                            return last

                        def first(g, b):
                            if kind == "gate":
                                ae.wait_ge(s_z, g + 1)
                                nc.scalar.activation(z[:, 1, :], z[:, 0, :], ACT.Sigmoid, bias=col[:, 1:2]
                                                     ).then_inc(s_gate, 1)
                                normalise(tm2, tmp, g * norms + 1, (b, 0), ACT.Identity).then_inc(s_n1, 1)
                            if norms:
                                ae.wait_ge(s_ht, g + 1)
                                normalise(hb[:, b], xin[:, b], g * norms + norms, (b, 1), ACT.Relu).then_inc(s_h, 1)

                        def second(g, b, i):
                            if cols:
                                ae.wait_ge(s_ht, g + 3)
                                ae.wait_ge(s_mm, g * GB + GB)
                                nc.scalar.activation(hT[:, 0:4 * P].rearrange("p (u n) -> p u n", n=P),
                                                     pH[:, 0:4, :], ACT.Copy)
                                nc.scalar.activation(hT[:, 4 * P:GB * P].rearrange("p (u n) -> p u n", n=P),
                                                     pH[:, 4:GB, :], ACT.Copy).then_inc(s_hT, 1)
                            if there(g, 2):
                                stage(g + 2)
                            if there(g, 1):
                                first(g + 1, 1 - b)

                        stage(0)
                        first(0, 0)
                        stage(1)
                        groups(ae, second)

                    @block.tensor
                    def _(pe):
                        def turn_sums(g):
                            pe.wait_ge(s_stage, g + 1)
                            pe.wait_ge(s_read, g + 1)
                            for u in range(GB):
                                for k in range(2):
                                    last = nc.tensor.matmul(pA[:, u, :], accs[:, k, u * P:(u + 1) * P], ident[:],
                                                            start=k == 0, stop=k == 1 and own is None)
                                if own is not None:
                                    last = nc.tensor.matmul(pA[:, u, :], ident[:],
                                                            own[:, bass.ds(g * GB + u, 1), :].rearrange("p b f -> p (b f)"),
                                                            start=False, stop=True)
                            last.then_inc(s_sums, 1)

                        def second(g, b, i):
                            if sums and there(g, 1):
                                turn_sums(g + 1)
                            if not cols:
                                return
                            pe.wait_ge(s_h, g + 1)
                            pe.wait_ge(s_hT, g + 1)
                            for u in range(GB):
                                last = nc.tensor.transpose(pH[:, u, :], hb[:, b, u, :], ident[:])
                            last.then_inc(s_ht, 1)
                            pe.wait_ge(s_hT, g + 2)
                            for u in range(GB):
                                pe.wait_ge(s_ev, g * GB + (RING if u < RING else u + 1))
                                nc.tensor.matmul(pG[:, u % RING, 0:cols], hT[:, u * P:(u + 1) * P], w_of[kind][:],
                                                 start=True, stop=True).then_inc(s_mm, 1)

                        if sums:
                            turn_sums(0)
                        groups(pe, second)

                    @block.vector
                    def _(dve):
                        steps = {"in": 3, "gate": 14, "gcn": 4, "mid": 0, "gat": 5, "out": 0}[kind]

                        def over_blocks(v):
                            return v.unsqueeze(1).to_broadcast([P, GB, F])

                        def moments(c, of, k, which):
                            b, m = which
                            rs, nb = rss[:, b, m], nbs[:, b, m]
                            for u in range(GB):
                                last = nc.vector.bn_stats(stats[:, u, :], of[:, u, :])
                            c.link(last)
                            nc.vector.memset(spacer[:], 0.0)
                            for u in range(GB):
                                last = nc.vector.bn_aggr(mv[:, u, :], stats[:, u, :])
                            c.link(last)
                            nc.vector.tensor_scalar(rs, mv[:, :, 1], 1e-5, None, ALU.add).then_inc(s_var, 1)
                            dve.wait_ge(s_std, k)
                            c.link(nc.vector.reciprocal(rs, rs))
                            nc.vector.scalar_tensor_tensor(nb, mv[:, :, 0], -1.0, rs, ALU.mult, ALU.mult
                                                           ).then_inc(s_nb, 1)

                        def first(g, b):
                            c = Chain(dve, s_c, g * steps)
                            xi = x_nat[:, bass.ds(g * GB, GB), :]
                            ki = keep[:, bass.ds(g * GB, GB), :]
                            agg = pA[:, 0:GB, :]
                            x_new = xin[:, b]
                            if sums:
                                dve.wait_ge(s_sums, g + 2)
                            if kind == "in":
                                nc.vector.tensor_scalar(x_new, xi, 0.0, None, ALU.add).then_inc(s_x, 1)
                                dve.wait_ge(s_x, g + 1)
                            if kind == "gate":
                                c.link(nc.vector.tensor_tensor(tmp[:], agg, over_blocks(wgs[:, 1, :]), ALU.mult))
                                dve.wait_ge(s_skip, g + 1)
                                c.link(nc.vector.tensor_tensor(tmp[:], tmp[:], gskip[:, b], ALU.add))
                                nc.vector.tensor_reduce(z[:, 0, :], tmp[:], AX, ALU.add).then_inc(s_z, 1)
                                c.link(nc.vector.tensor_tensor(tm2[:], ki, agg, ALU.subtract))
                                dve.wait_ge(s_gate, g + 1)
                                for u in range(GB):
                                    last = nc.vector.scalar_tensor_tensor(tmp[:, u, :], tm2[:, u, :], z[:, 1, u:u + 1],
                                                                          pA[:, u, :], ALU.mult, ALU.add)
                                last.then_inc(s_read, 1)
                                dve.wait_ge(s_read, g + 2)
                                moments(c, tmp, g * norms + 1, (b, 0))
                                dve.wait_ge(s_n1, g + 1)
                                c.link(nc.vector.tensor_tensor(tm2[:], tm2[:], over_blocks(row_of["gamma"][:]), ALU.mult))
                                c.link(nc.vector.tensor_tensor(tm2[:], tm2[:], over_blocks(row_of["beta"][:]), ALU.add))
                                c.link(nc.vector.tensor_scalar(tmp[:], tm2[:], 0.0, col[:, 2:3], ALU.min, ALU.mult))
                                c.link(nc.vector.scalar_tensor_tensor(tmp[:], tm2[:], 0.0, tmp[:], ALU.max, ALU.add))
                            if kind in ("gcn", "mid", "gat"):
                                to = hb[:, b] if kind == "mid" else tmp[:]
                                if kind == "mid":
                                    dve.wait_ge(s_ht, g + 1)
                                for u in range(GB):
                                    di = dinv[:, bass.ds(g * GB + ((0 if kind == "gcn" else NB) + u), 1)]
                                    last = nc.vector.scalar_tensor_tensor(to[:, u, :], pA[:, u, :], di,
                                                                          row_of[kind][:], ALU.mult, ALU.add)
                                last.then_inc(s_read, 1)
                                if kind == "mid":
                                    dve.wait_ge(s_read, g + 2)
                                    dve.sem_inc(s_h, 1)
                                    return
                                dve.wait_ge(s_read, g + 2)
                                if kind == "gat":
                                    c.link(nc.vector.scalar_tensor_tensor(tmp[:], tmp[:], 0.1, tmp[:], ALU.mult, ALU.max))
                            if kind == "out":
                                nc.vector.tensor_tensor(xi, agg, over_blocks(row_of["out"][:]), ALU.add).then_inc(s_x, 1)
                                dve.wait_ge(s_x, g + 1)
                                dve.sem_inc(s_read, 1)
                                return
                            if kind != "in":
                                c.link(nc.vector.tensor_tensor(x_new, xi, tmp[:], ALU.add))
                                nc.vector.tensor_scalar(xi, x_new, 0.0, None, ALU.add)
                            moments(c, x_new, g * norms + norms, (b, 1))
                            assert c.n == steps, (kind, c.n)

                        def second(g, b, i):
                            if there(g, 1):
                                first(g + 1, 1 - b)
                            if not cols:
                                return
                            if slabbed:
                                dve.wait_ge(s_st[b], i * (16 * len(stores)) + 16)
                            for u in range(GB):
                                dve.wait_ge(s_mm, g * GB + u + 1 + GB)
                                p = pG[:, u % RING, :]
                                mine = keep[:, bass.ds(g * GB + u, 1), :]
                                if kind == "in":
                                    nc.vector.tensor_tensor(slab[:, b, u, :], p[:, 0:3 * F], b_in[:, 0:3 * F], ALU.add)
                                    last = nc.vector.tensor_tensor(mine, p[:, 3 * F:4 * F].unsqueeze(1),
                                                                   b_in[:, 3 * F:4 * F].unsqueeze(1), ALU.add)
                                elif kind == "gate":
                                    nc.vector.tensor_tensor(slab[:, b, u, :], p[:, 0:F], b_gate[:], ALU.add)
                                    last = nc.vector.tensor_copy(mine, p[:, F:2 * F].unsqueeze(1))
                                elif kind in ("gcn", "mid"):
                                    last = nc.vector.tensor_scalar(mine, p[:, 0:F].unsqueeze(1),
                                                                   dinv[:, bass.ds(g * GB + (u + NB), 1)], None, ALU.mult)
                                else:
                                    last = nc.vector.tensor_copy(slab[:, b, u, :], p[:, 0:cols])
                                last.then_inc(s_ev, 1)

                        first(0, 0)
                        groups(dve, second)

        def scale_rows():
            with Phase(nc) as cx:
                s_sc = sem(cx, "sc_scaled")
                s_tb = sem(cx, "sc_stored")
                with nc.Block() as block:
                    @block.vector
                    def _(dve):
                        nc.vector.tensor_tensor(keep[:], keep[:], dinv[:, 0:NB].unsqueeze(2).to_broadcast([P, NB, F]),
                                                ALU.mult).then_inc(s_sc, 1)

                    @block.sync
                    def _(sp):
                        sp.wait_ge(s_sc, 1)
                        sp.dma_start(tab_row[0:NPAD, :].rearrange("(b p) f -> p b f", p=P), keep[:]).then_inc(s_tb, 16)
                        sp.wait_ge(s_tb, 16)

        node_phase("in")
        score_pass(0)
        softmax(0)
        aggregate("sum0", H, False)
        node_phase("gate")
        score_pass(1)
        scale_rows()
        aggregate("sum1", 1, True)
        node_phase("gcn")
        aggregate("sum2", None, True)
        node_phase("mid")
        aggregate("sum3", None, True)
        node_phase("gat")
        score_pass(3)
        softmax(3)
        aggregate("sum4", H, False)
        node_phase("out")


_WEIGHTS = ['L0_gnn_Wq', 'L0_gnn_bq', 'L0_gnn_Wk', 'L0_gnn_bk', 'L0_gnn_Wv', 'L0_gnn_bv', 'L0_gnn_Ws', 'L0_gnn_bs',
            'L0_gnn_Wg', 'L0_gnn_bg', 'L0_gnn_gamma', 'L0_gnn_beta', 'L0_gnn_alpha', 'L1_gnn_mlp_w1', 'L1_gnn_mlp_b1',
            'L1_gnn_mlp_w2', 'L1_gnn_mlp_b2', 'L1_gnn_conv_w', 'L1_gnn_conv_b', 'L2_gnn_W1', 'L2_gnn_b1', 'L2_gnn_W2',
            'L2_gnn_b2', 'L3_gnn_W', 'L3_gnn_a_l', 'L3_gnn_a_r', 'L3_gnn_bias']


def kernel(**inputs):
    import numpy as _np
    import concourse.bacc as _bacc
    from concourse import mybir as _mybir
    from concourse.bass_utils import run_bass_kernel_spmd as _run

    def by_tile(v, fill):
        line = _np.full(EP, fill, v.dtype)
        line[:E] = v
        return _np.ascontiguousarray(line.reshape(T, P).T)

    src, dst = _np.asarray(inputs["src"]), _np.asarray(inputs["dst"])
    line = _np.full((1, EP + 2), N, dst.dtype)
    line[0, 0] = line[0, -1] = -1
    line[0, 1:1 + E] = dst
    arrays = {"x": _np.ascontiguousarray(inputs["x"]), "src_pt": by_tile(src, 0), "dst_pt": by_tile(dst, N),
              "dst_line": line, "ew_pt": by_tile(_np.asarray(inputs["edge_weight"]), 0)}
    for name in _WEIGHTS:
        w = _np.ascontiguousarray(inputs[name])
        arrays[name] = w.reshape(1) if w.ndim == 0 else w
    nc = _bacc.Bacc("TRN2", target_bir_lowering=False, num_devices=1)
    args = {n: nc.dram_tensor("in_" + n, v.shape, _mybir.dt.from_np(v.dtype), kind="ExternalInput").ap()
            for n, v in arrays.items()}
    out = nc.dram_tensor("out_0", (N, F), _mybir.dt.float32, kind="ExternalOutput").ap()
    gnn_kernel(nc, args, out)
    r = _run(nc, [{"in_" + n: v for n, v in arrays.items()}], core_ids=[0])
    return r.results[0]["out_0"]
```

```python
import concourse.bass as bass
from concourse import mybir
from contextlib import ExitStack

fp32 = mybir.dt.float32
bf16 = mybir.dt.bfloat16
i32 = mybir.dt.int32
ALU = mybir.AluOpType
ACT = mybir.ActivationFunctionType
AX = mybir.AxisListType.X

P = 128
N = 6250
E = 106250
F = 128
H = 4
D = F // H
NB = -(-N // P)
NTAIL = N - (NB - 1) * P
NPAD = NB * P
TB = 8
T = -(-E // (P * 32)) * 32
EP = T * P
BATCHES = T // TB
ROUNDS = BATCHES // 2
ROWS = NPAD + P
GB = 7
GROUPS = NB // GB
DVE_TILES = 2
CH = 32
CT = T // CH
CE = CT * P
BIG = 1e30
SCALE = 1.0 / float(D) ** 0.5
assert NB % GB == 0 and T % CH == 0 and BATCHES % 2 == 0


class Chain:

    def __init__(self, eng, sem, start=0):
        self.eng, self.sem, self.start, self.n = eng, sem, start, 0

    def link(self, ins):
        self.n += 1
        ins.then_inc(self.sem, 1)
        self.eng.wait_ge(self.sem, self.start + self.n)


class Phase(ExitStack):

    def __init__(self, nc):
        super().__init__()
        self.nc, self.sems = nc, []

    def __exit__(self, *exc):
        if self.sems and exc[0] is None:
            self.nc.clear_and_free_semaphores(self.sems)
            self.nc.all_engine_barrier()
        return super().__exit__(*exc)


def gnn_kernel(nc, a, out):
    ctx = ExitStack()

    def sb(name, shape, dt=fp32, where=None):
        return (where or ctx).enter_context(nc.sbuf_tensor(name, shape, dt))

    def ps(where, name, shape):
        return where.enter_context(nc.psum_tensor(name, shape, fp32))

    def sem(where, name):
        s = nc.alloc_semaphore(name)
        where.sems.append(s)
        return s

    def dram(name, shape):
        return nc.dram_tensor(name, shape, fp32, kind="Internal").ap()

    tab_qv = dram("tab_qv", [ROWS, 2 * F])
    tab_k = dram("tab_k", [ROWS, F])
    tab_ax = dram("tab_ax", [ROWS, F // 2 + F])
    tab_b = dram("tab_b", [ROWS, F // 2])
    tab_row = dram("tab_row", [ROWS, F])
    tab_wh = dram("tab_wh", [ROWS, F + H])
    tab_er = dram("tab_er", [ROWS, H])
    spill = dram("spill", [P, T, F])
    src_lo = dram("src_lo", [1, EP])

    with ctx:
        x_nat = sb("x_nat", [P, NB, F])
        keep = sb("keep", [P, NB, F])
        acc = sb("acc", [P, 2, ROWS])
        score = sb("score", [P, H * T])
        local = sb("local", [P, T + TB])
        src_idx = sb("src_idx", [P, T], i32)
        base = sb("base", [1, T + TB], i32)
        iota = sb("iota", [P, P])
        ident = sb("ident", [P, P])
        dinv = sb("dinv", [P, 2 * NB])
        w_of = {k: sb("w_" + k, [P, n]) for k, n in (("in", 4 * F), ("gate", 2 * F), ("gcn", F), ("mid", F),
                                                     ("gat", F + 2 * H))}
        b_in = sb("b_in", [P, 4 * F])
        b_gate = sb("b_gate", [P, 2 * F])
        wg = sb("wg", [P, 3, F])
        wgs = sb("wgs", [P, 2, F])
        att = sb("att", [P, 2 * H])
        gatT = sb("gatT", [P, F])
        one = sb("one", [P, 1])
        minus_p = sb("minus_p", [P, 1])
        row_of = {k: sb("r_" + k, [P, F]) for k in ("gamma", "beta", "gcn", "mid", "gat", "out", "mlp")}
        col = sb("col", [P, 3])

        def of_batch(n):
            return score[:].rearrange("p (h t) -> p t h", h=H)[:, bass.ds(n * TB, TB), :]

        def bcast(v, n):
            return bass.AP(tensor=v.tensor, offset=v.offset, ap=[[0, P], [1, n]])

        with Phase(nc) as cx:
            dst_pt = sb("dst_pt", [P, T], i32, cx)
            base_all = sb("base_all", [P, T], i32, cx)
            zero = sb("zero", [P, 2 * F], fp32, cx)
            lo_i = sb("lo_i", [P, T], i32, cx)
            lo_f = sb("lo_f", [P, T], fp32, cx)
            s_in = sem(cx, "s_in")
            s_lo = sem(cx, "s_lo")
            s_lostored = sem(cx, "s_lostored")
            s_zero = sem(cx, "s_zero")
            s_pad = sem(cx, "s_pad")
            s_io = sem(cx, "s_io")
            s_set = sem(cx, "s_set")
            s_ld = sem(cx, "s_ld")
            s_att = sem(cx, "s_att")
            s_gatT = sem(cx, "s_gatT")
            s_gatc = sem(cx, "s_gatc")
            s_wa = sem(cx, "s_wa")
            pW = ps(cx, "pW", [P, 2, F])
            loads = [(w_of["in"][:, k * F:(k + 1) * F], a["L0_gnn_W" + c]) for k, c in enumerate("qvks")]
            loads += [(b_in[:, k * F:(k + 1) * F], bcast(a["L0_gnn_b" + c], F)) for k, c in enumerate("qvks")]
            loads += [(w_of["gate"][:, 0:F // 2], a["L1_gnn_mlp_w1"][0:F, :]),
                      (w_of["gate"][:, F // 2:F // 2 + F], a["L1_gnn_conv_w"]),
                      (w_of["gate"][:, F // 2 + F:2 * F], a["L1_gnn_mlp_w1"][F:2 * F, :]),
                      (b_gate[:, F // 2 + F:2 * F], bcast(a["L1_gnn_mlp_b1"], F // 2)),
                      (wg[:].rearrange("p k f -> p (k f)"), bcast(a["L0_gnn_Wg"], 3 * F)),
                      (col[:, 0:1], bcast(a["L1_gnn_mlp_b2"], 1)), (col[:, 1:2], bcast(a["L0_gnn_bg"], 1)),
                      (col[:, 2:3], bcast(a["L0_gnn_alpha"], 1)),
                      (row_of["mlp"][:, 0:F // 2], bcast(a["L1_gnn_mlp_w2"], F // 2)),
                      (row_of["gamma"][:], bcast(a["L0_gnn_gamma"], F)),
                      (row_of["beta"][:], bcast(a["L0_gnn_beta"], F)),
                      (w_of["gcn"][:], a["L2_gnn_W1"]), (row_of["gcn"][:], bcast(a["L1_gnn_conv_b"], F)),
                      (w_of["mid"][:], a["L2_gnn_W2"]), (row_of["mid"][:], bcast(a["L2_gnn_b1"], F)),
                      (row_of["gat"][:], bcast(a["L2_gnn_b2"], F)),
                      (row_of["out"][:], bcast(a["L3_gnn_bias"], F))]
            loads += [(w_of["gat"][:, h * D:(h + 1) * D], a["L3_gnn_W"][h]) for h in range(H)]
            with nc.Block() as block:
                @block.sync
                def _(sp):
                    sp.dma_start(dst_pt[:], a["dst_pt"]).then_inc(s_in, 16)
                    sp.dma_start(base_all[:], bass.AP(tensor=a["dst_pt"].tensor, offset=0, ap=[[0, P], [1, T]])
                                 ).then_inc(s_in, 16)
                    sp.dma_start(src_idx[:], a["src_pt"]).then_inc(s_in, 16)
                    sp.dma_start(lo_i[:], a["src_run"]).then_inc(s_lo, 16)
                    sp.wait_ge(s_zero, 1)
                    sp.dma_start(x_nat[:, 0:NB - 1, :], a["x"][0:(NB - 1) * P, :].rearrange("(b p) f -> p b f", p=P)
                                 ).then_inc(s_in, 16)
                    sp.dma_start(x_nat[0:NTAIL, NB - 1, :], a["x"][(NB - 1) * P:N, :]).then_inc(s_in, 16)
                    sp.wait_ge(s_zero, 1)
                    for to, of in loads:
                        sp.dma_start(to, of).then_inc(s_ld, 16)
                    for k, name in enumerate(("L3_gnn_a_l", "L3_gnn_a_r")):
                        for h in range(H):
                            sp.dma_start(att[h * D:(h + 1) * D, k * H + h:k * H + h + 1], a[name][h]).then_inc(s_att, 16)
                    tabs = (tab_qv, tab_k, tab_ax, tab_b, tab_row, tab_wh, tab_er)
                    for t in tabs:
                        sp.dma_start(t[NPAD:ROWS, :], zero[:, 0:t.shape[1]]).then_inc(s_pad, 16)
                    sp.wait_ge(s_lo, 18)
                    sp.dma_start(src_lo.rearrange("o (p t) -> (o p) t", t=T), lo_f[:]).then_inc(s_lostored, 16)
                    sp.wait_ge(s_lostored, 16)
                    sp.wait_ge(s_ld, 16 * len(loads))
                    sp.wait_ge(s_att, 16 * 2 * H)
                    sp.wait_ge(s_pad, 16 * len(tabs))
                    sp.wait_ge(s_in, 16 * 5)

                @block.gpsimd
                def _(pool):
                    nc.gpsimd.iota(iota[:], [[1, P]], base=0, channel_multiplier=0,
                                   allow_small_or_imprecise_dtypes=True).then_inc(s_io, 1)
                    nc.gpsimd.iota(minus_p[:], [[0, 1]], base=0, channel_multiplier=-1,
                                   allow_small_or_imprecise_dtypes=True)
                    nc.gpsimd.memset(ident[:], 0.0).then_inc(s_io, 1)
                    pool.wait_ge(s_io, 2)
                    nc.gpsimd.affine_select(out=ident[:], in_=ident[:], compare_op=ALU.not_equal, fill=1.0,
                                            base=0, pattern=[[-1, P]], channel_multiplier=1).then_inc(s_io, 1)

                @block.vector
                def _(dve):
                    nc.vector.memset(x_nat[:, NB - 1, :], 0.0)
                    nc.vector.memset(att[:], 0.0)
                    nc.vector.memset(b_gate[:], 0.0)
                    nc.vector.memset(zero[:], 0.0).then_inc(s_zero, 1)
                    nc.vector.memset(local[:], 0.0)
                    nc.vector.memset(base[:], 0)
                    nc.vector.memset(one[:], 1.0).then_inc(s_set, 1)
                    dve.wait_ge(s_lo, 16)
                    nc.vector.tensor_scalar(lo_i[:], lo_i[:], P - 1, None, ALU.bitwise_and).then_inc(s_lo, 1)
                    dve.wait_ge(s_lo, 17)
                    nc.vector.tensor_copy(lo_f[:], lo_i[:]).then_inc(s_lo, 1)
                    dve.wait_ge(s_in, 16 * 5)
                    dve.wait_ge(s_set, 1)
                    nc.vector.tensor_tensor(local[:, 0:T], dst_pt[:], base_all[:], ALU.subtract)
                    nc.vector.tensor_copy(base[0:1, 0:T], dst_pt[0:1, :])
                    dve.wait_ge(s_ld, 16 * len(loads))
                    nc.vector.tensor_tensor(wgs[:, 0, :], wg[:, 0, :], wg[:, 2, :], ALU.add)
                    nc.vector.tensor_tensor(wgs[:, 1, :], wg[:, 1, :], wg[:, 2, :], ALU.subtract)
                    dve.wait_ge(s_gatT, 1)
                    nc.vector.tensor_copy(gatT[:], pW[:, 0, :]).then_inc(s_gatc, 1)
                    dve.wait_ge(s_wa, 1)
                    nc.vector.tensor_copy(w_of["gat"][:, F:F + 2 * H], pW[:, 1, 0:2 * H])

                @block.tensor
                def _(pe):
                    pe.wait_ge(s_ld, 16 * len(loads))
                    pe.wait_ge(s_io, 3)
                    nc.tensor.transpose(pW[:, 0, :], w_of["gat"][:, 0:F], ident[:]).then_inc(s_gatT, 1)
                    pe.wait_ge(s_gatc, 1)
                    pe.wait_ge(s_att, 16 * 2 * H)
                    nc.tensor.matmul(pW[:, 1, 0:2 * H], gatT[:], att[:], start=True, stop=True).then_inc(s_wa, 1)

        def onehot(dst, n, tiles=TB):
            return nc.vector.tensor_tensor(dst, iota[:].unsqueeze(1).to_broadcast([P, tiles, P]),
                                           local[:, bass.ds(n * TB, tiles)].unsqueeze(2).to_broadcast([P, tiles, P]),
                                           ALU.is_equal)

        def score_pass(layer):
            table, win = {0: (tab_qv, tab_k), 1: (tab_ax, tab_b), 3: (tab_wh, tab_er)}[layer]
            RW, WW = table.shape[1], win.shape[1]
            v0 = {0: F, 1: F // 2, 3: 0}[layer]
            with Phase(nc) as cx:
                L = f"l{layer}_"
                idx = sb(L + "idx", [P, 2 * TB], i32, cx)
                rows = sb(L + "rows", [P, 2 * TB, RW], fp32, cx)
                hot = sb(L + "hot", [P, 2, TB, P], fp32, cx)
                hotT = sb(L + "hotT", [P, 2, TB, P], fp32, cx)
                winr = sb(L + "winr", [P, 2 * TB, WW], fp32, cx)
                pT = ps(cx, L + "pT", [P, TB, P])
                pK = ps(cx, L + "pK", [P, 2, TB, max(WW, F // 2)])[:, :, :, 0:WW]
                s_rows = [sem(cx, L + f"s_rows{b}") for b in range(2)]
                s_win = [sem(cx, L + f"s_win{b}") for b in range(2)]
                s_spill = [sem(cx, L + f"s_spill{b}") for b in range(2)]
                s_idx = sem(cx, L + "s_idx")
                s_used = sem(cx, L + "s_used")
                s_hot = sem(cx, L + "s_hot")
                s_tr = sem(cx, L + "s_tr")
                s_hotT = sem(cx, L + "s_hotT")
                s_dst = sem(cx, L + "s_dst")
                s_chain = sem(cx, L + "s_chain")
                if layer == 1:
                    pre = sb(L + "pre", [P, 2, TB, WW], fp32, cx)
                    act = sb(L + "act", [P, 2, TB, WW], fp32, cx)
                    logit = sb(L + "logit", [P, 2, TB], fp32, cx)
                    lo = sb(L + "lo", [P, 2, TB, P], fp32, cx)
                    hi = sb(L + "hi", [P, 2, TB, 2 * NB], fp32, cx)
                    dst_i = sb(L + "dst_i", [P, T], i32, cx)
                    dst_d = sb(L + "dst_d", [P, T], i32, cx)
                    dlo, dhi = acc[:, 0, 0:T], acc[:, 1, 0:T]
                    zer = sb(L + "zer", [P, P], fp32, cx)
                    pD = ps(cx, L + "pD", [P, 2 * NB])
                    s_dl = sem(cx, L + "s_dl")
                    s_split = sem(cx, L + "s_split")
                    s_pre = s_used
                    s_act = sem(cx, L + "s_act")
                    s_logit = sem(cx, L + "s_logit")
                    s_edge = sem(cx, L + "s_edge")
                    s_hi = sem(cx, L + "s_hi")
                    s_count = sem(cx, L + "s_count")
                    s_deg = sem(cx, L + "s_deg")
                    s_dend = sem(cx, L + "s_dend")
                    s_sqrt = sem(cx, L + "s_sqrt")
                    s_zer = sem(cx, L + "s_zer")
                if layer == 0:
                    prod = sb(L + "prod", [P, 2, TB, F], fp32, cx)
                if layer == 3:
                    lin = sb(L + "lin", [P, 2, TB, H], fp32, cx)
                    lnw = sb(L + "lnw", [P, T], fp32, cx)
                    s_ew = sem(cx, L + "s_ew")
                    s_lin = sem(cx, L + "s_lin")
                    s_lnc = sem(cx, L + "s_lnc")
                    s_lnw = sem(cx, L + "s_lnw")

                with nc.Block() as block:
                    @block.sync
                    def _(sp):
                        if layer == 1:
                            sp.dma_start(dst_i[:], a["dst_pt"]).then_inc(s_dl, 16)
                            sp.sem_inc(s_deg, 2)
                        if layer == 3:
                            sp.dma_start(lnw[:], a["ew_pt"]).then_inc(s_ew, 16)
                        sp.sem_inc(s_dst, 2)
                        for b in range(2):
                            sp.sem_inc(s_spill[b], 16)
                        regs = [sp.alloc_register(L + f"win{u}") for u in range(TB)]

                        def load_windows(n, b):
                            sp.load(regs, base[0:1, bass.ds(n * TB, TB)])
                            sp.wait_ge(s_dst, n + 1)
                            for u in range(TB):
                                at = sp.snap(regs[u], min_val=0, max_val=N)
                                sp.dma_start(winr[:, b * TB + u, :], win[bass.ds(at, P), :]).then_inc(s_win[b], 16)

                        def store_values(n, b, i):
                            sp.wait_ge(s_rows[b], i * (16 * TB) + 16 * TB)
                            sp.dma_start(spill[:, bass.ds(n * TB, TB), :], rows[:, b * TB:(b + 1) * TB, v0:v0 + F]
                                         ).then_inc(s_spill[b], 16)

                        load_windows(0, 0)
                        with sp.Fori(0, ROUNDS) as i:
                            for b in range(2):
                                load_windows(i * 2 + b + 1, 1 - b)
                                store_values(i * 2 + b, b, i)
                        for b in range(2):
                            sp.wait_ge(s_spill[b], 16 * (ROUNDS + 1))
                        sp.wait_ge(s_win[0], 16 * TB * (ROUNDS + 1))

                    @block.gpsimd
                    def _(pool):
                        pool.sem_inc(s_used, 2)
                        with pool.Fori(0, ROUNDS) as i:
                            for b in range(2):
                                pool.wait_ge(s_used, i * 2 + b + 1)
                                pool.wait_ge(s_spill[b], i * 16 + 16)
                                nc.gpsimd.tensor_copy(idx[:, b * TB:(b + 1) * TB],
                                                      src_idx[:, bass.ds((i * 2 + b) * TB, TB)]).then_inc(s_idx, 1)
                                pool.wait_ge(s_idx, 1)
                                pool.wait_ge(s_idx, i * 2 + b + 1)
                                for u in range(b * TB, (b + 1) * TB):
                                    nc.gpsimd.indirect_dma_start(
                                        rows[:, u, :], None, table,
                                        bass.IndirectOffsetOnAxis(idx[:, u:u + 1], 0)).then_inc(s_rows[b], 16)

                    @block.tensor
                    def _(pe):
                        def turn(n, b):
                            pe.wait_ge(s_hot, n + 1)
                            for u in range(TB):
                                last = nc.tensor.transpose(pT[:, u, :], hot[:, b, u, :], ident[:])
                            last.then_inc(s_tr, 1)

                        def spread(n, b, i):
                            pe.wait_ge(s_win[b], i * (16 * TB) + 16 * TB)
                            pe.wait_ge(s_used, n + 1)
                            for u in range(TB):
                                last = nc.tensor.matmul(pK[:, b, u, :], hotT[:, b, u, :], winr[:, b * TB + u, :],
                                                        start=True, stop=True)
                            last.then_inc(s_dst, 1)

                        def degrees(n, b):
                            pe.wait_ge(s_hi, n + 1)
                            for u in range(TB):
                                last = nc.tensor.matmul(pD[:], lo[:, b, u, :], hi[:, b, u, :], start=False, stop=False)
                            last.then_inc(s_deg, 1)

                        def step(n, b, i):
                            pe.wait_ge(s_hotT, n + 1)
                            spread(n, b, i)
                            turn(n + 1, 1 - b)

                        if layer == 1:
                            pe.wait_ge(s_zer, 1)
                            nc.tensor.matmul(pD[:], zer[:], zer[:, 0:2 * NB], start=True, stop=False)
                        turn(0, 0)
                        step(0, 0, 0)
                        step(1, 1, 0)
                        with pe.Fori(0, ROUNDS - 1) as i:
                            for b in range(2):
                                step(i * 2 + b + 2, b, i + 1)
                                if layer == 1:
                                    degrees(i * 2 + b, b)
                        if layer == 1:
                            degrees(BATCHES - 2, 0)
                            degrees(BATCHES - 1, 1)
                            nc.tensor.matmul(pD[:], zer[:], zer[:, 0:2 * NB], start=False, stop=True
                                             ).then_inc(s_dend, 1)

                    @block.scalar
                    def _(act_e):
                        def copy_turned(n, b):
                            act_e.wait_ge(s_tr, n + 2)
                            act_e.wait_ge(s_dst, n + 1)
                            nc.scalar.activation(hotT[:, b, 0:4, :], pT[:, 0:4, :], ACT.Copy)
                            nc.scalar.activation(hotT[:, b, 4:8, :], pT[:, 4:8, :], ACT.Copy).then_inc(s_hotT, 1)

                        if layer == 3:
                            act_e.wait_ge(s_lnc, 1)
                            nc.scalar.activation(lnw[:], lnw[:], ACT.Ln).then_inc(s_lnw, 1)
                        copy_turned(0, 0)
                        with act_e.Fori(0, ROUNDS) as i:
                            for b in range(2):
                                n = i * 2 + b
                                if layer == 1:
                                    act_e.wait_ge(s_pre, n + 3)
                                    nc.scalar.activation(act[:, b], pre[:, b], ACT.Gelu).then_inc(s_act, 1)
                                copy_turned(n + 1, 1 - b)
                                if layer == 1:
                                    act_e.wait_ge(s_logit, n + 1)
                                    nc.scalar.activation(score[:, bass.ds(n * TB, TB)], logit[:, b], ACT.Sigmoid,
                                                         bias=col[:, 0:1]).then_inc(s_edge, 1)
                        if layer == 1:
                            act_e.wait_ge(s_dend, 2)
                            nc.scalar.activation(dinv[:], dinv[:], ACT.Sqrt).then_inc(s_sqrt, 1)

                    @block.vector
                    def _(dve):
                        if layer == 1:
                            nc.vector.memset(zer[:], 0.0).then_inc(s_zer, 1)
                            dve.wait_ge(s_dl, 16)
                            pc = Chain(dve, s_split)
                            pc.link(nc.vector.tensor_scalar(dst_d[:], dst_i[:], P - 1, None, ALU.bitwise_and))
                            pc.link(nc.vector.tensor_copy(dlo, dst_d[:]))
                            pc.link(nc.vector.tensor_scalar(dst_d[:], dst_i[:], 7, None, ALU.logical_shift_right))
                            pc.link(nc.vector.tensor_copy(dhi, dst_d[:]))
                        if layer == 3:
                            dve.wait_ge(s_ew, 16)
                            nc.vector.tensor_scalar(lnw[:], lnw[:], 1e-8, None, ALU.max).then_inc(s_lnc, 1)
                            dve.wait_ge(s_lnw, 1)
                        dve.sem_inc(s_tr, 1)
                        onehot(hot[:, 0], 0).then_inc(s_hot, 1)

                        def meet(n, b, i):
                            rb = rows[:, b * TB:(b + 1) * TB, :]
                            dve.wait_ge(s_tr, n + 1)
                            onehot(hot[:, 1 - b], n + 1).then_inc(s_hot, 1)
                            dve.wait_ge(s_dst, n + 3)
                            dve.wait_ge(s_rows[b], i * (16 * TB) + 16 * TB)
                            if layer == 0:
                                for g in range(2):
                                    nc.vector.tensor_tensor(prod[:, b, 4 * g:4 * g + 4, :], rb[:, 4 * g:4 * g + 4, 0:F],
                                                            pK[:, b, 4 * g:4 * g + 4, :], ALU.mult).then_inc(s_chain, 1)
                                dve.wait_ge(s_chain, 2)
                                dve.wait_ge(s_chain, n * 2 + 2)
                                nc.vector.tensor_reduce(
                                    of_batch(n), prod[:, b].rearrange("p t (h d) -> p t h d", d=D), AX, ALU.add
                                ).then_inc(s_used, 1)
                            if layer == 1:
                                nc.vector.tensor_tensor(pre[:, b], rb[:, :, 0:WW], pK[:, b], ALU.add).then_inc(s_pre, 1)
                            if layer == 3:
                                nc.vector.tensor_tensor(lin[:, b], rb[:, :, F:F + H], pK[:, b], ALU.add
                                                        ).then_inc(s_chain, 1)
                                dve.wait_ge(s_chain, n * 2 + 1)
                                nc.vector.scalar_tensor_tensor(lin[:, b], lin[:, b], 0.2, lin[:, b],
                                                               ALU.mult, ALU.max).then_inc(s_chain, 1)
                                dve.wait_ge(s_chain, n * 2 + 2)
                                nc.vector.tensor_tensor(
                                    of_batch(n), lin[:, b],
                                    lnw[:, bass.ds(n * TB, TB)].unsqueeze(2).to_broadcast([P, TB, H]), ALU.add
                                ).then_inc(s_used, 1)

                        def mlp_out(n, b):
                            dve.wait_ge(s_act, n + 1)
                            nc.vector.tensor_tensor(act[:, b], act[:, b],
                                                    row_of["mlp"][:, 0:WW].unsqueeze(1).to_broadcast([P, TB, WW]), ALU.mult
                                                    ).then_inc(s_chain, 1)
                            dve.wait_ge(s_chain, n + 1)
                            nc.vector.tensor_reduce(logit[:, b], act[:, b], AX, ALU.add).then_inc(s_logit, 1)

                        def degree_operands(n, b):
                            dve.wait_ge(s_deg, n + 1)
                            nc.vector.tensor_tensor(
                                lo[:, b], iota[:].unsqueeze(1).to_broadcast([P, TB, P]),
                                dlo[:, bass.ds(n * TB, TB)].unsqueeze(2).to_broadcast([P, TB, P]), ALU.is_equal)
                            nc.vector.tensor_tensor(
                                hi[:, b, :, NB:2 * NB], iota[:, 0:NB].unsqueeze(1).to_broadcast([P, TB, NB]),
                                dhi[:, bass.ds(n * TB, TB)].unsqueeze(2).to_broadcast([P, TB, NB]),
                                ALU.is_equal).then_inc(s_count, 1)
                            dve.wait_ge(s_edge, n + 1)
                            dve.wait_ge(s_count, n + 1)
                            nc.vector.tensor_tensor(
                                hi[:, b, :, 0:NB], hi[:, b, :, NB:2 * NB],
                                score[:, bass.ds(n * TB, TB)].unsqueeze(2).to_broadcast([P, TB, NB]),
                                ALU.mult).then_inc(s_hi, 1)

                        if layer == 1:
                            meet(0, 0, 0)
                            mlp_out(0, 0)
                            with dve.Fori(0, ROUNDS - 1) as i:
                                meet(i * 2 + 1, 1, i)
                                degree_operands(i * 2, 0)
                                mlp_out(i * 2 + 1, 1)
                                meet(i * 2 + 2, 0, i + 1)
                                degree_operands(i * 2 + 1, 1)
                                mlp_out(i * 2 + 2, 0)
                            meet(BATCHES - 1, 1, ROUNDS - 1)
                            degree_operands(BATCHES - 2, 0)
                            mlp_out(BATCHES - 1, 1)
                            degree_operands(BATCHES - 1, 1)
                        else:
                            with dve.Fori(0, ROUNDS) as i:
                                for b in range(2):
                                    meet(i * 2 + b, b, i)
                        if layer == 1:
                            dve.wait_ge(s_dend, 1)
                            nc.vector.tensor_scalar(dinv[:], pD[:], 1.0, None, ALU.add).then_inc(s_dend, 1)
                            dve.wait_ge(s_sqrt, 1)
                            nc.vector.reciprocal(dinv[:], dinv[:])

        def softmax(layer):
            scale, eps = (SCALE, 0.0) if layer == 0 else (1.0, 1e-8)
            with Phase(nc) as cx:
                L = f"x{layer}_"
                dchunk = sb(L + "dchunk", [P, CE + 2], i32, cx)
                room = acc[:].rearrange("p k n -> p (k n)")
                same = room[:, 0:CE + 1]
                brk = room[:, CE + 1:2 * CE + 2]
                lg = sb(L + "lg", [P, CE], fp32, cx)
                fw = room[:, 2 * CE + 2:3 * CE + 2]
                bw = sb(L + "bw", [P, CE], fp32, cx)
                whole = sb(L + "whole", [P, 2], fp32, cx)
                rowg = sb(L + "rowg", [1, 2, P], fp32, cx)
                rowp = sb(L + "rowp", [1, 2, P], fp32, cx)
                carry = sb(L + "carry", [1, 4, P + 1], fp32, cx)
                init = sb(L + "init", [P, 4], fp32, cx)
                pB = ps(cx, L + "pB", [P, CT, P])
                pR = ps(cx, L + "pR", [P, 4 * P])
                s_dc = sem(cx, L + "s_dc")
                s_turn = sem(cx, L + "s_turn")
                s_lg = sem(cx, L + "s_lg")
                s_whole = sem(cx, L + "s_whole")
                s_rowg = sem(cx, L + "s_rowg")
                s_end = sem(cx, L + "s_end")
                s_row = sem(cx, L + "s_row")
                s_car = sem(cx, L + "s_car")
                s_init = sem(cx, L + "s_init")
                s_c = sem(cx, L + "s_c")
                s_exp = sem(cx, L + "s_exp")
                s_diff = sem(cx, L + "s_diff")
                s_w = sem(cx, L + "s_w")
                s_back = sem(cx, L + "s_back")
                by_chunk = score[:].rearrange("p (q j) -> p j q", j=CT)
                ends = [(fw, CE - 1), (bw, 0), (fw, CE - 1), (bw, 0)]
                with nc.Block() as block:
                    @block.sync
                    def _(sp):
                        for h in range(H):
                            sp.dma_start(dchunk[h * CH:(h + 1) * CH, :],
                                         bass.AP(tensor=a["dst_line"].tensor, offset=0, ap=[[CE, CH], [1, CE + 2]])
                                         ).then_inc(s_dc, 16)
                        sp.wait_ge(s_dc, 16 * H)

                    @block.tensor
                    def _(pe):
                        for j in range(CT):
                            last = nc.tensor.transpose(pB[:, j, :], by_chunk[:, j], ident[:])
                        last.then_inc(s_turn, 1)
                        pe.wait_ge(s_whole, 1)
                        for k in range(2):
                            last = nc.tensor.matmul(pR[0:1, k * P:(k + 1) * P], whole[:, k:k + 1], ident[:],
                                                    start=True, stop=True)
                        last.then_inc(s_rowg, 1)
                        for k, (buf, at) in enumerate(ends):
                            pe.wait_ge(s_end, k + 1)
                            nc.tensor.matmul(pR[0:1, 2 * P:3 * P], buf[:, at:at + 1], ident[:], start=True, stop=True
                                             ).then_inc(s_row, 1)
                            pe.wait_ge(s_car, k + 1)
                            o = k % 2
                            nc.tensor.matmul(pR[:, 3 * P:3 * P + 1], carry[0:1, k, o:o + P], one[0:1, :],
                                             start=True, stop=True).then_inc(s_init, 1)
                        pe.wait_ge(s_w, 1)
                        for j in range(CT):
                            last = nc.tensor.transpose(pB[:, j, :], lg[:, j * P:(j + 1) * P], ident[:])
                        last.then_inc(s_back, 1)

                    @block.scalar
                    def _(act_e):
                        act_e.wait_ge(s_turn, 1)
                        for j in range(0, CT, 4):
                            m = min(4, CT - j)
                            last = nc.scalar.activation(lg[:, j * P:(j + m) * P].rearrange("p (j e) -> p j e", e=P),
                                                        pB[:, j:j + m, :], ACT.Copy)
                        last.then_inc(s_lg, 1)
                        act_e.wait_ge(s_diff, 1)
                        nc.scalar.activation(lg[:], lg[:], ACT.Exp, scale=scale).then_inc(s_exp, 1)
                        act_e.wait_ge(s_back, 1)
                        for j in range(0, CT, 4):
                            m = min(4, CT - j)
                            nc.scalar.activation(by_chunk[:, j:j + m], pB[:, j:j + m, :], ACT.Copy)

                    @block.vector
                    def _(dve):
                        c = Chain(dve, s_c)
                        dve.wait_ge(s_dc, 16 * H)
                        c.link(nc.vector.tensor_tensor(same, dchunk[:, 0:CE + 1], dchunk[:, 1:CE + 2], ALU.is_equal))
                        nc.vector.tensor_reduce(whole[:, 0:1], same[:, 0:CE], AX, ALU.min)
                        nc.vector.tensor_reduce(whole[:, 1:2], same[:, 1:CE + 1], AX, ALU.min).then_inc(s_whole, 1)
                        nc.vector.tensor_scalar(brk, same, 1.0, BIG, ALU.subtract, ALU.mult)
                        nc.vector.memset(carry[:], -BIG)
                        dve.wait_ge(s_rowg, 1)
                        c.link(nc.vector.tensor_copy(rowg[:].rearrange("p k n -> p (k n)"), pR[0:1, 0:2 * P]))
                        c.link(nc.vector.tensor_scalar(rowp[:], rowg[:], 1.0, BIG, ALU.subtract, ALU.mult))
                        c.link(nc.vector.memset(carry[:, 2, :], 0.0))

                        def segment_scan(k, out, data, marks, rows_, op0, op1, start):
                            back = k % 2
                            m = marks[:, 1:CE + 1] if back else marks[:, 0:CE]
                            rev = (lambda ap: ap[:, ::-1]) if back else (lambda ap: ap)
                            nc.vector.tensor_tensor_scan(rev(out), rev(m), rev(data), start, op0, op1
                                                         ).then_inc(s_end, 1)
                            dve.wait_ge(s_row, k + 1)
                            row = pR[0:1, 2 * P:3 * P]
                            to = carry[:, k, 0:P] if back else carry[:, k, 1:P + 1]
                            nc.vector.tensor_tensor_scan(rev(to), rev(rows_[:, back, :]), rev(row), start, op0, op1
                                                         ).then_inc(s_car, 1)
                            dve.wait_ge(s_init, k + 1)
                            c.link(nc.vector.tensor_copy(init[:, k:k + 1], pR[:, 3 * P:3 * P + 1]))
                            c.link(nc.vector.tensor_tensor_scan(rev(out), rev(m), rev(data), init[:, k:k + 1],
                                                                op0, op1))

                        dve.wait_ge(s_lg, 1)
                        segment_scan(0, fw, lg[:], brk, rowp, ALU.add, ALU.max, -BIG)
                        segment_scan(1, bw[:], fw, brk, rowp, ALU.add, ALU.max, -BIG)
                        nc.vector.tensor_tensor(lg[:], lg[:], bw[:], ALU.subtract).then_inc(s_diff, 1)
                        dve.wait_ge(s_exp, 1)
                        segment_scan(2, fw, lg[:], same, rowg, ALU.mult, ALU.add, 0.0)
                        segment_scan(3, bw[:], fw, brk, rowp, ALU.add, ALU.max, -BIG)
                        if eps:
                            c.link(nc.vector.tensor_scalar(bw[:], bw[:], eps, None, ALU.add))
                        c.link(nc.vector.reciprocal(bw[:], bw[:]))
                        nc.vector.tensor_tensor(lg[:], lg[:], bw[:], ALU.mult).then_inc(s_w, 1)

        def aggregate(name, weights):
            gather = weights is None
            with Phase(nc) as cx:
                L = name + "_"
                hot = sb(L + "hot", [P, 2, TB, P], fp32, cx)
                rows = sb(L + "rows", [P, 2 * TB, F], fp32, cx)
                idx = sb(L + "idx", [P, 2 * TB], i32, cx)
                wrow = rows if gather else sb(L + "wrow", [P, 2 * TB, F], fp32, cx)
                pA = ps(cx, L + "pA", [P, 2, TB, P])
                s_rows = [sem(cx, L + f"s_rows{b}") for b in range(2)]
                s_idx = sem(cx, L + "s_idx")
                s_hot = sem(cx, L + "s_hot")
                by_dve = TB if gather else DVE_TILES
                s_square = sem(cx, L + "s_square")
                s_hot_act = sem(cx, L + "s_hot_act")
                s_wrow = sem(cx, L + "s_wrow")
                s_sum = sem(cx, L + "s_sum")
                s_free = s_sum if gather else s_wrow
                s_add = sem(cx, L + "s_add")
                if weights == "edge":
                    line = sb(L + "line", [P, 2, TB * P], fp32, cx)
                    hot_lo = sb(L + "hot_lo", [P, 2, TB * P], bf16, cx)
                    hot_hi = sb(L + "hot_hi", [P, 2, TB, NB], fp32, cx)
                    hi_i = sb(L + "hi_i", [P, T], i32, cx)
                    hi_f = score[:, T:2 * T]
                    wedge = sb(L + "wedge", [P, 2, TB], fp32, cx)
                    pS = ps(cx, L + "pS", [P, 2, TB, F // 2])[:, :, :, 0:NB]
                    s_line = [sem(cx, L + f"s_line{b}") for b in range(2)]
                    s_dist = sem(cx, L + "s_dist")
                    s_lo = sem(cx, L + "s_lo")
                    s_look = sem(cx, L + "s_look")
                    part = sb(L + "part", [P, 3, NB], bf16, cx)
                    rest = sb(L + "rest", [P, 2, NB], fp32, cx)
                    s_split = sem(cx, L + "s_split")
                    s_hi = sem(cx, L + "s_hi")
                    s_pick = sem(cx, L + "s_pick")
                    s_picked = sem(cx, L + "s_picked")
                    s_wedge = sem(cx, L + "s_wedge")

                def weigh(n, b):
                    half = slice(b * TB, (b + 1) * TB)
                    if weights == "head":
                        return nc.gpsimd.tensor_tensor(wrow[:, half, :].rearrange("p t (h d) -> p t h d", d=D),
                                                       rows[:, half, :].rearrange("p t (h d) -> p t h d", d=D),
                                                       of_batch(n).unsqueeze(3).to_broadcast([P, TB, H, D]), ALU.mult)
                    return nc.gpsimd.tensor_tensor(wrow[:, half, :], rows[:, half, :],
                                                   wedge[:, b].unsqueeze(2).to_broadcast([P, TB, F]), ALU.mult)

                with nc.Block() as block:
                    @block.gpsimd
                    def _(pool):
                        pool.sem_inc(s_wrow, 2)
                        if not gather:
                            with pool.Fori(0, ROUNDS) as i:
                                for b in range(2):
                                    if weights == "edge":
                                        pool.wait_ge(s_wedge, i * 2 + b + 1)
                                    pool.wait_ge(s_sum, i * 2 + b + 1)
                                    pool.wait_ge(s_rows[b], 16)
                                    pool.wait_ge(s_rows[b], i * 16 + 16)
                                    weigh(i * 2 + b, b).then_inc(s_wrow, 1)
                        if gather:
                            with pool.Fori(0, ROUNDS) as i:
                                for b in range(2):
                                    pool.wait_ge(s_free, i * 2 + b + 1)
                                    nc.gpsimd.tensor_copy(idx[:, b * TB:(b + 1) * TB],
                                                          src_idx[:, bass.ds((i * 2 + b) * TB, TB)]).then_inc(s_idx, 1)
                                    pool.wait_ge(s_idx, 1)
                                    pool.wait_ge(s_idx, i * 2 + b + 1)
                                    for u in range(b * TB, (b + 1) * TB):
                                        nc.gpsimd.indirect_dma_start(
                                            rows[:, u, :], None, tab_row,
                                            bass.IndirectOffsetOnAxis(idx[:, u:u + 1], 0)).then_inc(s_rows[b], 16)

                    @block.sync
                    def _(sp):
                        if not gather:
                            with sp.Fori(0, ROUNDS) as i:
                                for b in range(2):
                                    sp.wait_ge(s_free, i * 2 + b + 1)
                                    sp.dma_start(rows[:, b * TB:(b + 1) * TB, :],
                                                 spill[:, bass.ds((i * 2 + b) * TB, TB), :]).then_inc(s_rows[b], 16)

                    @block.tensor
                    def _(pe):
                        def look_up(n, b):
                            pe.wait_ge(s_lo, n + 1)
                            pe.wait_ge(s_picked, n + 1)
                            for u in range(TB):
                                for k in range(3):
                                    last = nc.tensor.matmul(pS[:, b, u, :], hot_lo[:, b, u * P:(u + 1) * P],
                                                            part[:, k, :], start=k == 0, stop=k == 2)
                            last.then_inc(s_look, 1)

                        def sum_up(n, b, i):
                            pe.wait_ge(s_hot, n + 1)
                            if gather:
                                pe.wait_ge(s_rows[b], i * (16 * TB) + 16 * TB)
                            else:
                                pe.wait_ge(s_hot_act, n + 1)
                                pe.wait_ge(s_wrow, n + 3)
                            for u in range(TB):
                                last = nc.tensor.matmul(pA[:, b, u, :], wrow[:, b * TB + u, :], hot[:, b, u, :],
                                                        start=True, stop=True)
                            last.then_inc(s_sum, 1)

                        if weights == "edge":
                            pe.sem_inc(s_picked, 2)
                            pe.wait_ge(s_split, 7)
                            look_up(0, 0)
                            with pe.Fori(0, ROUNDS - 1) as i:
                                look_up(i * 2 + 1, 1)
                                sum_up(i * 2, 0, i)
                                look_up(i * 2 + 2, 0)
                                sum_up(i * 2 + 1, 1, i)
                            look_up(BATCHES - 1, 1)
                            sum_up(BATCHES - 2, 0, ROUNDS - 1)
                            sum_up(BATCHES - 1, 1, ROUNDS - 1)
                        else:
                            with pe.Fori(0, ROUNDS) as i:
                                for b in range(2):
                                    sum_up(i * 2 + b, b, i)

                    @block.scalar
                    def _(act_e):
                        def hot_part(n, b):
                            act_e.wait_ge(s_sum, n + 1)
                            for u in range(by_dve, TB):
                                last = nc.scalar.activation(hot[:, b, u, :], iota[:], ACT.Square, scale=-1.0,
                                                            bias=local[:, bass.ds(n * TB + u, 1)])
                            last.then_inc(s_square, 1)
                            act_e.wait_ge(s_square, n + 1)
                            nc.scalar.activation(hot[:, b, by_dve:TB, :], hot[:, b, by_dve:TB, :], ACT.Relu,
                                                 scale=-1.0, bias=one[:]).then_inc(s_hot_act, 1)

                        if weights == "head":
                            with act_e.Fori(0, ROUNDS) as i:
                                for b in range(2):
                                    hot_part(i * 2 + b, b)
                        if weights == "edge":
                            def load_line(n, b):
                                nc.scalar.dma_start(line[:, b, :], bass.AP(
                                    tensor=src_lo.tensor, offset=n * (TB * P), ap=[[0, P], [1, TB * P]])
                                ).then_inc(s_line[b], 16)

                            def hot_low(n, b, i, more):
                                act_e.wait_ge(s_line[b], i * 16 + 16)
                                act_e.wait_ge(s_look, n + 1)
                                nc.scalar.activation(hot_lo[:, b], line[:, b], ACT.Square, bias=minus_p[:]
                                                     ).then_inc(s_dist, 1)
                                act_e.wait_ge(s_dist, n + 1)
                                nc.scalar.activation(hot_lo[:, b], hot_lo[:, b], ACT.Relu, scale=-1.0, bias=one[:]
                                                     ).then_inc(s_lo, 1)
                                if more:
                                    load_line(n + 2, b)
                                hot_part(n, b)

                            act_e.sem_inc(s_look, 2)
                            for b in range(2):
                                load_line(b, b)
                            with act_e.Fori(0, ROUNDS - 1) as i:
                                for b in range(2):
                                    hot_low(i * 2 + b, b, i, True)
                            for b in range(2):
                                hot_low(BATCHES - 2 + b, b, ROUNDS - 1, False)

                    @block.vector
                    def _(dve):
                        regs = [dve.alloc_register(L + f"at{u}") for u in range(TB)]

                        def prepare(n, b):
                            dve.wait_ge(s_sum, n + 1)
                            onehot(hot[:, b, 0:by_dve, :], n, by_dve).then_inc(s_hot, 1)
                            if weights == "edge":
                                nc.vector.tensor_tensor(
                                    hot_hi[:, b], iota[:, 0:NB].unsqueeze(1).to_broadcast([P, TB, NB]),
                                    hi_f[:, bass.ds(n * TB, TB)].unsqueeze(2).to_broadcast([P, TB, NB]),
                                    ALU.is_equal).then_inc(s_hi, 1)
                                dve.wait_ge(s_look, n + 3)
                                dve.wait_ge(s_hi, n + 1)
                                nc.vector.tensor_tensor(hot_hi[:, b], hot_hi[:, b], pS[:, b], ALU.mult
                                                        ).then_inc(s_pick, 1)
                                dve.wait_ge(s_pick, n + 1)
                                dve.wait_ge(s_wrow, n + 1)
                                nc.vector.tensor_reduce(wedge[:, b], hot_hi[:, b], AX, ALU.add).then_inc(s_picked, 1)
                                dve.wait_ge(s_picked, n + 3)
                                nc.vector.tensor_tensor(wedge[:, b], wedge[:, b], score[:, bass.ds(n * TB, TB)],
                                                        ALU.mult).then_inc(s_wedge, 1)

                        def add_windows(n, b):
                            dve.load(regs, base[0:1, bass.ds(n * TB, TB)])
                            dve.wait_ge(s_sum, n + 3)
                            for u in range(TB):
                                at = dve.snap(regs[u], min_val=0, max_val=N)
                                dve.wait_ge(s_add, n * TB + u + 1)
                                nc.vector.tensor_tensor(acc[:, u % 2, bass.ds(at, P)], acc[:, u % 2, bass.ds(at, P)],
                                                        pA[:, b, u, :], ALU.add).then_inc(s_add, 1)

                        dve.sem_inc(s_sum, 2)
                        if weights == "edge":
                            c = Chain(dve, s_split)
                            c.link(nc.vector.tensor_copy(part[:, 0, :], dinv[:, 0:NB]))
                            c.link(nc.vector.tensor_tensor(rest[:, 0, :], dinv[:, 0:NB], part[:, 0, :], ALU.subtract))
                            c.link(nc.vector.tensor_copy(part[:, 1, :], rest[:, 0, :]))
                            c.link(nc.vector.tensor_tensor(rest[:, 1, :], rest[:, 0, :], part[:, 1, :], ALU.subtract))
                            c.link(nc.vector.tensor_copy(part[:, 2, :], rest[:, 1, :]))
                            c.link(nc.vector.tensor_scalar(hi_i[:], src_idx[:], 7, None, ALU.logical_shift_right))
                            c.link(nc.vector.tensor_copy(hi_f, hi_i[:]))
                        nc.vector.memset(acc[:], 0.0).then_inc(s_add, 2)
                        prepare(0, 0)
                        with dve.Fori(0, ROUNDS - 1) as i:
                            prepare(i * 2 + 1, 1)
                            add_windows(i * 2, 0)
                            prepare(i * 2 + 2, 0)
                            add_windows(i * 2 + 1, 1)
                        prepare(BATCHES - 1, 1)
                        add_windows(BATCHES - 2, 0)
                        add_windows(BATCHES - 1, 1)

        def node_phase(kind):
            cols = w_of[kind].shape[1] if kind in w_of else 0
            sums = kind != "in"
            own = {"gcn": keep, "mid": keep, "gat": keep, "out": x_nat}.get(kind)
            norms = {"gate": 2, "mid": 0, "out": 0}.get(kind, 1)
            slabbed = kind in ("in", "gate", "gat")
            SW = {"in": 3 * F, "gate": 2 * F, "gat": F + 2 * H}.get(kind, 1)
            RING = 4
            with Phase(nc) as cx:
                L = kind + "_"
                xin = sb(L + "xin", [P, 2, GB, F], fp32, cx)
                hb = sb(L + "hb", [P, 2, GB, F], fp32, cx)
                tmp = sb(L + "tmp", [P, GB, F], fp32, cx)
                tm2 = sb(L + "tm2", [P, GB, F], fp32, cx)
                gskip = sb(L + "gskip", [P, 2, GB, F], fp32, cx) if kind == "gate" else None
                accs = sb(L + "accs", [P, 2, GB * P], fp32, cx)
                hT = sb(L + "hT", [P, GB * P], fp32, cx)
                stats = sb(L + "stats", [P, GB, 6], fp32, cx)
                mv = sb(L + "mv", [P, GB, 2], fp32, cx)
                rss = sb(L + "rss", [P, 2, 2, GB], fp32, cx)
                nbs = sb(L + "nbs", [P, 2, 2, GB], fp32, cx)
                spacer = sb(L + "spacer", [P, 1], fp32, cx)
                z = sb(L + "z", [P, 2, GB], fp32, cx)
                slab = sb(L + "slab", [P, 2, GB, SW], fp32, cx)
                pA = ps(cx, L + "pA", [P, 8, P])
                pH = ps(cx, L + "pH", [P, 8, P])
                pG = ps(cx, L + "pG", [P, RING, 4 * F])
                s_c = sem(cx, L + "s_c")
                s_stage = sem(cx, L + "s_stage")
                s_sums = sem(cx, L + "s_sums")
                s_read = sem(cx, L + "s_read")
                s_var = sem(cx, L + "s_var")
                s_std = sem(cx, L + "s_std")
                s_nb = sem(cx, L + "s_nb")
                s_n1 = sem(cx, L + "s_n1")
                s_z = sem(cx, L + "s_z")
                s_gate = sem(cx, L + "s_gate")
                s_skip = sem(cx, L + "s_skip")
                s_h = sem(cx, L + "s_h")
                s_ht = sem(cx, L + "s_ht")
                s_hT = sem(cx, L + "s_hT")
                s_mm = sem(cx, L + "s_mm")
                s_ev = sem(cx, L + "s_ev")
                s_st = [sem(cx, L + f"s_st{b}") for b in range(2)]
                s_x = sem(cx, L + "s_x")

                def rows_of(table, g, c0, c1):
                    return table[0:NPAD, c0:c1].rearrange("(b p) c -> p b c", p=P)[:, bass.ds(g * GB, GB), :]

                stores = {"in": [(tab_qv, 0, 2 * F, 0), (tab_k, 0, F, 2 * F)],
                          "gate": [(tab_ax, 0, F // 2 + F, 0), (tab_b, 0, F // 2, F // 2 + F)],
                          "gcn": [(tab_row, 0, F, 0)], "mid": [(tab_row, 0, F, 0)],
                          "gat": [(tab_wh, 0, F + H, 0), (tab_er, 0, H, F + H)], "out": []}[kind]

                def groups(eng, body):
                    with eng.Fori(0, (GROUPS - 3) // 2) as i:
                        for b in range(2):
                            body(i * 2 + b, b, i)
                    for g in range(GROUPS - 3, GROUPS):
                        body(g, g % 2, g // 2)

                def there(g, n=0):
                    return not isinstance(g, int) or g + n < GROUPS

                assert GROUPS % 2 == 1
                with nc.Block() as block:
                    @block.sync
                    def _(sp):
                        sp.sem_inc(s_st[0], 16)
                        sp.sem_inc(s_st[1], 16)
                        sp.sem_inc(s_ht, 2)
                        sp.sem_inc(s_hT, 1)
                        sp.sem_inc(s_mm, GB)
                        sp.sem_inc(s_sums, 1)
                        sp.sem_inc(s_read, 1)
                        sp.sem_inc(s_ev, RING)

                        def store(g, b, i):
                            if kind == "out":
                                sp.wait_ge(s_x, g + 1)
                                if there(g, 1):
                                    sp.dma_start(out[0:(NB - 1) * P, :].rearrange("(b p) f -> p b f", p=P)
                                                 [:, bass.ds(g * GB, GB), :],
                                                 x_nat[:, bass.ds(g * GB, GB), :]).then_inc(s_st[b], 16)
                                else:
                                    sp.dma_start(out[g * GB * P:(NB - 1) * P, :].rearrange("(b p) f -> p b f", p=P),
                                                 x_nat[:, g * GB:NB - 1, :]).then_inc(s_st[b], 16)
                                    sp.dma_start(out[(NB - 1) * P:N, :], x_nat[0:NTAIL, NB - 1, :]
                                                 ).then_inc(s_st[1 - b], 16)
                                return
                            sp.wait_ge(s_ev, g * GB + GB + RING)
                            for table, c0, c1, at in stores:
                                of = slab[:, b, :, at:at + c1 - c0] if slabbed else keep[:, bass.ds(g * GB, GB), :]
                                sp.dma_start(rows_of(table, g, c0, c1), of).then_inc(s_st[b], 16)

                        groups(sp, store)
                        m = max(len(stores), 1)
                        sp.wait_ge(s_st[0], 16 + 16 * m * (GROUPS + 1) // 2)
                        sp.wait_ge(s_st[1], 16 + 16 * m * (GROUPS // 2) + (16 if kind == "out" else 0))

                    @block.gpsimd
                    def _(pool):
                        if kind == "gate":
                            def skip_part(g, b, i):
                                pool.wait_ge(s_read, 1)
                                pool.wait_ge(s_read, g + 1)
                                nc.gpsimd.tensor_tensor(gskip[:, b], keep[:, bass.ds(g * GB, GB), :],
                                                        wgs[:, 0, :].unsqueeze(1).to_broadcast([P, GB, F]), ALU.mult
                                                        ).then_inc(s_skip, 1)
                            groups(pool, skip_part)

                    @block.scalar
                    def _(ae):
                        def stage(g):
                            if sums:
                                ae.wait_ge(s_sums, g + 1)
                                nc.scalar.activation(accs[:], acc[:, :, bass.ds(g * (GB * P), GB * P)], ACT.Copy
                                                     ).then_inc(s_stage, 1)

                        def normalise(to, of, k, which, func):
                            b, m = which
                            rs, nb = rss[:, b, m], nbs[:, b, m]
                            ae.wait_ge(s_var, k)
                            nc.scalar.activation(rs, rs, ACT.Sqrt).then_inc(s_std, 1)
                            ae.wait_ge(s_nb, k)
                            for u in range(GB):
                                last = nc.scalar.activation(to[:, u, :], of[:, u, :], func, scale=rs[:, u:u + 1],
                                                            bias=nb[:, u:u + 1])
                            return last

                        def first(g, b):
                            if kind == "gate":
                                ae.wait_ge(s_z, g + 1)
                                nc.scalar.activation(z[:, 1, :], z[:, 0, :], ACT.Sigmoid, bias=col[:, 1:2]
                                                     ).then_inc(s_gate, 1)
                                normalise(tm2, tmp, g * norms + 1, (b, 0), ACT.Identity).then_inc(s_n1, 1)
                            if norms:
                                ae.wait_ge(s_ht, g + 1)
                                normalise(hb[:, b], xin[:, b], g * norms + norms, (b, 1), ACT.Relu).then_inc(s_h, 1)

                        def second(g, b, i):
                            if cols:
                                ae.wait_ge(s_ht, g + 3)
                                ae.wait_ge(s_mm, g * GB + GB)
                                nc.scalar.activation(hT[:, 0:4 * P].rearrange("p (u n) -> p u n", n=P),
                                                     pH[:, 0:4, :], ACT.Copy)
                                nc.scalar.activation(hT[:, 4 * P:GB * P].rearrange("p (u n) -> p u n", n=P),
                                                     pH[:, 4:GB, :], ACT.Copy).then_inc(s_hT, 1)
                            if there(g, 2):
                                stage(g + 2)
                            if there(g, 1):
                                first(g + 1, 1 - b)

                        stage(0)
                        first(0, 0)
                        stage(1)
                        groups(ae, second)

                    @block.tensor
                    def _(pe):
                        def turn_sums(g):
                            pe.wait_ge(s_stage, g + 1)
                            pe.wait_ge(s_read, g + 1)
                            for u in range(GB):
                                for k in range(2):
                                    last = nc.tensor.matmul(pA[:, u, :], accs[:, k, u * P:(u + 1) * P], ident[:],
                                                            start=k == 0, stop=k == 1 and own is None)
                                if own is not None:
                                    last = nc.tensor.matmul(pA[:, u, :], ident[:],
                                                            own[:, bass.ds(g * GB + u, 1), :].rearrange("p b f -> p (b f)"),
                                                            start=False, stop=True)
                            last.then_inc(s_sums, 1)

                        def second(g, b, i):
                            if sums and there(g, 1):
                                turn_sums(g + 1)
                            if not cols:
                                return
                            pe.wait_ge(s_h, g + 1)
                            pe.wait_ge(s_hT, g + 1)
                            for u in range(GB):
                                last = nc.tensor.transpose(pH[:, u, :], hb[:, b, u, :], ident[:])
                            last.then_inc(s_ht, 1)
                            pe.wait_ge(s_hT, g + 2)
                            for u in range(GB):
                                pe.wait_ge(s_ev, g * GB + (RING if u < RING else u + 1))
                                nc.tensor.matmul(pG[:, u % RING, 0:cols], hT[:, u * P:(u + 1) * P], w_of[kind][:],
                                                 start=True, stop=True).then_inc(s_mm, 1)

                        if sums:
                            turn_sums(0)
                        groups(pe, second)

                    @block.vector
                    def _(dve):
                        steps = {"in": 3, "gate": 14, "gcn": 4, "mid": 0, "gat": 5, "out": 0}[kind]

                        def over_blocks(v):
                            return v.unsqueeze(1).to_broadcast([P, GB, F])

                        def moments(c, of, k, which):
                            b, m = which
                            rs, nb = rss[:, b, m], nbs[:, b, m]
                            for u in range(GB):
                                last = nc.vector.bn_stats(stats[:, u, :], of[:, u, :])
                            c.link(last)
                            nc.vector.memset(spacer[:], 0.0)
                            for u in range(GB):
                                last = nc.vector.bn_aggr(mv[:, u, :], stats[:, u, :])
                            c.link(last)
                            nc.vector.tensor_scalar(rs, mv[:, :, 1], 1e-5, None, ALU.add).then_inc(s_var, 1)
                            dve.wait_ge(s_std, k)
                            c.link(nc.vector.reciprocal(rs, rs))
                            nc.vector.scalar_tensor_tensor(nb, mv[:, :, 0], -1.0, rs, ALU.mult, ALU.mult
                                                           ).then_inc(s_nb, 1)

                        def first(g, b):
                            c = Chain(dve, s_c, g * steps)
                            xi = x_nat[:, bass.ds(g * GB, GB), :]
                            ki = keep[:, bass.ds(g * GB, GB), :]
                            agg = pA[:, 0:GB, :]
                            x_new = xin[:, b]
                            if sums:
                                dve.wait_ge(s_sums, g + 2)
                            if kind == "in":
                                nc.vector.tensor_scalar(x_new, xi, 0.0, None, ALU.add).then_inc(s_x, 1)
                                dve.wait_ge(s_x, g + 1)
                            if kind == "gate":
                                c.link(nc.vector.tensor_tensor(tmp[:], agg, over_blocks(wgs[:, 1, :]), ALU.mult))
                                dve.wait_ge(s_skip, g + 1)
                                c.link(nc.vector.tensor_tensor(tmp[:], tmp[:], gskip[:, b], ALU.add))
                                nc.vector.tensor_reduce(z[:, 0, :], tmp[:], AX, ALU.add).then_inc(s_z, 1)
                                c.link(nc.vector.tensor_tensor(tm2[:], ki, agg, ALU.subtract))
                                dve.wait_ge(s_gate, g + 1)
                                for u in range(GB):
                                    last = nc.vector.scalar_tensor_tensor(tmp[:, u, :], tm2[:, u, :], z[:, 1, u:u + 1],
                                                                          pA[:, u, :], ALU.mult, ALU.add)
                                last.then_inc(s_read, 1)
                                dve.wait_ge(s_read, g + 2)
                                moments(c, tmp, g * norms + 1, (b, 0))
                                dve.wait_ge(s_n1, g + 1)
                                c.link(nc.vector.tensor_tensor(tm2[:], tm2[:], over_blocks(row_of["gamma"][:]), ALU.mult))
                                c.link(nc.vector.tensor_tensor(tm2[:], tm2[:], over_blocks(row_of["beta"][:]), ALU.add))
                                c.link(nc.vector.tensor_scalar(tmp[:], tm2[:], 0.0, col[:, 2:3], ALU.min, ALU.mult))
                                c.link(nc.vector.scalar_tensor_tensor(tmp[:], tm2[:], 0.0, tmp[:], ALU.max, ALU.add))
                            if kind in ("gcn", "mid", "gat"):
                                to = hb[:, b] if kind == "mid" else tmp[:]
                                if kind == "mid":
                                    dve.wait_ge(s_ht, g + 1)
                                for u in range(GB):
                                    di = dinv[:, bass.ds(g * GB + ((0 if kind == "gcn" else NB) + u), 1)]
                                    last = nc.vector.scalar_tensor_tensor(to[:, u, :], pA[:, u, :], di,
                                                                          row_of[kind][:], ALU.mult, ALU.add)
                                last.then_inc(s_read, 1)
                                if kind == "mid":
                                    dve.wait_ge(s_read, g + 2)
                                    dve.sem_inc(s_h, 1)
                                    return
                                dve.wait_ge(s_read, g + 2)
                                if kind == "gat":
                                    c.link(nc.vector.scalar_tensor_tensor(tmp[:], tmp[:], 0.1, tmp[:], ALU.mult, ALU.max))
                            if kind == "out":
                                nc.vector.tensor_tensor(xi, agg, over_blocks(row_of["out"][:]), ALU.add).then_inc(s_x, 1)
                                dve.wait_ge(s_x, g + 1)
                                dve.sem_inc(s_read, 1)
                                return
                            if kind != "in":
                                c.link(nc.vector.tensor_tensor(x_new, xi, tmp[:], ALU.add))
                                nc.vector.tensor_scalar(xi, x_new, 0.0, None, ALU.add)
                            moments(c, x_new, g * norms + norms, (b, 1))
                            assert c.n == steps, (kind, c.n)

                        def second(g, b, i):
                            if there(g, 1):
                                first(g + 1, 1 - b)
                            if not cols:
                                return
                            if slabbed:
                                dve.wait_ge(s_st[b], i * (16 * len(stores)) + 16)
                            for u in range(GB):
                                dve.wait_ge(s_mm, g * GB + u + 1 + GB)
                                p = pG[:, u % RING, :]
                                mine = keep[:, bass.ds(g * GB + u, 1), :]
                                if kind == "in":
                                    nc.vector.tensor_tensor(slab[:, b, u, :], p[:, 0:3 * F], b_in[:, 0:3 * F], ALU.add)
                                    last = nc.vector.tensor_tensor(mine, p[:, 3 * F:4 * F].unsqueeze(1),
                                                                   b_in[:, 3 * F:4 * F].unsqueeze(1), ALU.add)
                                elif kind == "gate":
                                    nc.vector.tensor_tensor(slab[:, b, u, :], p[:, 0:2 * F], b_gate[:], ALU.add)
                                    last = nc.vector.tensor_copy(mine, p[:, F // 2:F // 2 + F].unsqueeze(1))
                                elif kind in ("gcn", "mid"):
                                    last = nc.vector.tensor_scalar(mine, p[:, 0:F].unsqueeze(1),
                                                                   dinv[:, bass.ds(g * GB + (u + NB), 1)], None, ALU.mult)
                                else:
                                    last = nc.vector.tensor_copy(slab[:, b, u, :], p[:, 0:cols])
                                last.then_inc(s_ev, 1)

                        first(0, 0)
                        groups(dve, second)

        def scale_rows():
            with Phase(nc) as cx:
                s_sc = sem(cx, "sc_scaled")
                with nc.Block() as block:
                    @block.vector
                    def _(dve):
                        nc.vector.tensor_tensor(keep[:], keep[:], dinv[:, 0:NB].unsqueeze(2).to_broadcast([P, NB, F]),
                                                ALU.mult).then_inc(s_sc, 1)
                        dve.wait_ge(s_sc, 1)

        node_phase("in")
        score_pass(0)
        softmax(0)
        aggregate("sum0", "head")
        node_phase("gate")
        score_pass(1)
        scale_rows()
        aggregate("sum1", "edge")
        node_phase("gcn")
        aggregate("sum2", None)
        node_phase("mid")
        aggregate("sum3", None)
        node_phase("gat")
        score_pass(3)
        softmax(3)
        aggregate("sum4", "head")
        node_phase("out")


_WEIGHTS = ['L0_gnn_Wq', 'L0_gnn_bq', 'L0_gnn_Wk', 'L0_gnn_bk', 'L0_gnn_Wv', 'L0_gnn_bv', 'L0_gnn_Ws', 'L0_gnn_bs',
            'L0_gnn_Wg', 'L0_gnn_bg', 'L0_gnn_gamma', 'L0_gnn_beta', 'L0_gnn_alpha', 'L1_gnn_mlp_w1', 'L1_gnn_mlp_b1',
            'L1_gnn_mlp_w2', 'L1_gnn_mlp_b2', 'L1_gnn_conv_w', 'L1_gnn_conv_b', 'L2_gnn_W1', 'L2_gnn_b1', 'L2_gnn_W2',
            'L2_gnn_b2', 'L3_gnn_W', 'L3_gnn_a_l', 'L3_gnn_a_r', 'L3_gnn_bias']


def kernel(**inputs):
    import numpy as _np
    import concourse.bacc as _bacc
    from concourse import mybir as _mybir
    from concourse.bass_utils import run_bass_kernel_spmd as _run

    def by_tile(v, fill):
        line = _np.full(EP, fill, v.dtype)
        line[:E] = v
        return _np.ascontiguousarray(line.reshape(T, P).T)

    src, dst = _np.asarray(inputs["src"]), _np.asarray(inputs["dst"])
    line = _np.full((1, EP + 2), N, dst.dtype)
    line[0, 0] = line[0, -1] = -1
    line[0, 1:1 + E] = dst
    src_pt = by_tile(src, 0)
    arrays = {"x": _np.ascontiguousarray(inputs["x"]), "src_pt": src_pt, "dst_pt": by_tile(dst, N),
              "src_run": _np.ascontiguousarray(src_pt.T).reshape(P, T),
              "dst_line": line, "ew_pt": by_tile(_np.asarray(inputs["edge_weight"]), 0)}
    for name in _WEIGHTS:
        w = _np.ascontiguousarray(inputs[name])
        arrays[name] = w.reshape(1) if w.ndim == 0 else w
    nc = _bacc.Bacc("TRN2", target_bir_lowering=False, num_devices=1)
    args = {n: nc.dram_tensor("in_" + n, v.shape, _mybir.dt.from_np(v.dtype), kind="ExternalInput").ap()
            for n, v in arrays.items()}
    out = nc.dram_tensor("out_0", (N, F), _mybir.dt.float32, kind="ExternalOutput").ap()
    gnn_kernel(nc, args, out)
    r = _run(nc, [{"in_" + n: v for n, v in arrays.items()}], core_ids=[0])
    return r.results[0]["out_0"]
```
